# Optimizing a Trainium2 kernel written in Bass

```python
import numpy as np
import jax
import jax.numpy as jnp

def _softmax(x, axis=-1):
    return jax.nn.softmax(x, axis=axis)

def _gelu(x):
    return jax.nn.gelu(x, approximate=True)

def _silu(x):
    return jax.nn.silu(x)

def _sigmoid(x):
    return jax.nn.sigmoid(x)

def _layernorm(x, axis=-1, eps=1e-05):
    m = jnp.mean(x, axis=axis, keepdims=True)
    v = jnp.var(x, axis=axis, keepdims=True)
    return (x - m) / jnp.sqrt(v + eps)

def _scatter_add(tgt, idx, src, axis=0):
    return tgt.at[idx].add(src)

def _segment_sum(src, seg, n):
    return jax.ops.segment_sum(src, seg, n)
kernel_name = 'mk_gnn_resnorm_d2_gnn_r32_15f1af'

def setup_inputs(seed: int=0):
    np.random.seed(seed)
    _w = jnp.asarray

    def _rec_inputs():
        import jax
        import jax.numpy as jnp
        _gk = jax.random.key(seed)
        x = -0.0007083 + 1.001 * jax.random.normal(jax.random.fold_in(_gk, 1), (3125, 48), jnp.float32)
        _s = jax.random.randint(jax.random.fold_in(_gk, 2), (50000,), 0, 3125, jnp.int32)
        _d = jax.random.randint(jax.random.fold_in(_gk, 3), (50000,), 0, 3125, jnp.int32)
        _loop = jnp.arange(3125, dtype=jnp.int32)
        src = jnp.concatenate([_s, _d, _loop])
        dst = jnp.concatenate([_d, _s, _loop])
        _o = jnp.argsort(dst, stable=True)
        src = src[_o]
        dst = dst[_o]
        edge_attr_40 = jax.random.uniform(jax.random.fold_in(_gk, 12), (103125, 40), jnp.float32, 0.0, 1)
        edge_weight = jax.random.uniform(jax.random.fold_in(_gk, 14), (103125,), jnp.float32, 0.0, 6.99999)
        node_type_119 = jax.random.randint(jax.random.fold_in(_gk, 15), (3125,), 0, 119, jnp.int32)
        node_vec = jax.random.uniform(jax.random.fold_in(_gk, 16), (3125,), jnp.float32, 0.0, 1.49999)
        return (x, src, dst, edge_attr_40, edge_weight, node_type_119, node_vec)
    x, src, dst, edge_attr_40, edge_weight, node_type_119, node_vec = _rec_inputs()

    def _L0_gnn_setup():
        import jax, jax.numpy as jnp
        import numpy as np
        CUTOFF = 6.0
        LN_EPS = 1e-05
        key = jax.random.key(seed)
        ks = jax.random.split(key, 16)
        N, E, H, R, NEL, G = (50000, 25000, 48, 40, 119, 32)
        inp = {'h': jax.random.normal(ks[0], (N, H), jnp.float32), 'edge_index': jax.random.randint(ks[1], (2, E), 0, N, jnp.int64), 'edge_attr': jax.random.uniform(ks[2], (E, R), jnp.float32), 'distances': jax.random.uniform(ks[3], (E,), jnp.float32) * 7.0, 'atom_z': jax.random.randint(ks[4], (N,), 0, NEL, jnp.int64), 'node_mult': jax.random.uniform(ks[5], (N,), jnp.float32) + 0.5, 'batch': jnp.zeros((N,), jnp.int64), 'W1': jax.random.normal(ks[6], (H, R), jnp.float32) / np.sqrt(R), 'b1': jax.random.normal(ks[7], (H,), jnp.float32) * 0.01, 'W2': jax.random.normal(ks[8], (H, H), jnp.float32) / np.sqrt(H), 'b2': jax.random.normal(ks[9], (H,), jnp.float32) * 0.01, 'emb': jax.random.normal(ks[10], (NEL, G), jnp.float32) * 0.01, 'adaptW': jax.random.normal(ks[11], (G, G), jnp.float32) * 0.01, 'gamma': jnp.ones((H,), jnp.float32), 'beta': jnp.zeros((H,), jnp.float32)}
        return inp
    _L0_gnn_all = _L0_gnn_setup()
    _L0_gnn_in = {k: v for k, v in _L0_gnn_all.items() if k in ('W1', 'b1', 'W2', 'b2', 'emb', 'adaptW', 'gamma', 'beta')}
    del _L0_gnn_all

    def _L1_gnn_setup():
        import jax, jax.numpy as jnp
        import numpy as np
        N_NODES = 50000
        N_EDGES = 50000
        D_IN = 48
        D_OUT = 48
        K = 4
        key = jax.random.key(seed)
        k1, k2, k3, k4, k5 = jax.random.split(key, 5)
        x = jax.random.normal(k1, (N_NODES, D_IN), dtype=jnp.float32)
        edge_index = jax.random.randint(k2, (2, N_EDGES), 0, N_NODES, dtype=jnp.int64)
        weight = jax.random.normal(k3, (K, D_IN, D_OUT), dtype=jnp.float32) * (1.0 / np.sqrt(D_IN))
        bias = jax.random.normal(k4, (D_OUT,), dtype=jnp.float32) * 0.01
        return {'x': x, 'edge_index': edge_index, 'weight': weight, 'bias': bias}
    _L1_gnn_all = _L1_gnn_setup()
    _L1_gnn_in = {k: v for k, v in _L1_gnn_all.items() if k in ('weight', 'bias')}
    del _L1_gnn_all
    return {'x': x, 'src': src, 'dst': dst, 'edge_attr_40': edge_attr_40, 'edge_weight': edge_weight, 'node_type_119': node_type_119, 'node_vec': node_vec, 'L0_gnn_W1': _L0_gnn_in['W1'], 'L0_gnn_b1': _L0_gnn_in['b1'], 'L0_gnn_W2': _L0_gnn_in['W2'], 'L0_gnn_b2': _L0_gnn_in['b2'], 'L0_gnn_emb': _L0_gnn_in['emb'], 'L0_gnn_adaptW': _L0_gnn_in['adaptW'], 'L0_gnn_gamma': _L0_gnn_in['gamma'], 'L0_gnn_beta': _L0_gnn_in['beta'], 'L1_gnn_weight': _L1_gnn_in['weight'], 'L1_gnn_bias': _L1_gnn_in['bias']}

def reference(x, src, dst, edge_attr_40, edge_weight, node_type_119, node_vec, L0_gnn_W1, L0_gnn_b1, L0_gnn_W2, L0_gnn_b2, L0_gnn_emb, L0_gnn_adaptW, L0_gnn_gamma, L0_gnn_beta, L1_gnn_weight, L1_gnn_bias):
    import jax
    import jax.numpy as jnp

    def _L0_gnn_ref(h, edge_index, edge_attr, distances, atom_z, node_mult, batch, W1, b1, W2, b2, emb, adaptW, gamma, beta):
        import jax, jax.numpy as jnp
        import numpy as np
        CUTOFF = 6.0
        LN_EPS = 1e-05
        src, dst = (edge_index[0], edge_index[1])
        N = h.shape[0]
        gate = jax.nn.silu(edge_attr @ W1.T + b1) @ W2.T + b2
        ei = emb[atom_z[src]]
        ej = emb[atom_z[dst]]
        adapt_logit = jnp.sum(ei * (ej @ adaptW.T), axis=-1, keepdims=True)
        gate = gate + adapt_logit
        cw = jnp.where(distances < CUTOFF, 0.5 * (jnp.cos(jnp.pi * distances / CUTOFF) + 1.0), 0.0)
        mj = node_mult[dst]
        msg = gate * h[dst] * (cw * mj)[:, None]
        agg = jax.ops.segment_sum(msg, src, num_segments=N)
        tot = jax.ops.segment_sum(mj, src, num_segments=N)
        agg = agg / jnp.clip(tot, 1e-08, None)[:, None]
        x = h + agg
        mu = jnp.mean(x, axis=-1, keepdims=True)
        var = jnp.mean(jnp.square(x - mu), axis=-1, keepdims=True)
        return (x - mu) / jnp.sqrt(var + LN_EPS) * gamma + beta

    def _L1_gnn_ref(x, edge_index, weight, bias):
        import jax, jax.numpy as jnp
        import numpy as np
        N_NODES = 50000
        N_EDGES = 50000
        D_IN = 48
        D_OUT = 48
        K = 4
        'PyG ChebConv forward with sym normalization, lambda_max=2.0.\n\n            L_hat = 2L/lambda_max - I. With lambda_max=2 and sym Laplacian, the\n            diagonal becomes 0 and off-diagonal weights are -d_i^{-1/2} d_j^{-1/2}.\n            T0 = x, T1 = L_hat x, Tk = 2 L_hat T_{k-1} - T_{k-2};  out = sum_k Tk W_k + b.\n            '
        n = x.shape[0]
        row, col = (edge_index[0], edge_index[1])
        ew = (row != col).astype(x.dtype)
        deg = jax.ops.segment_sum(ew, row, num_segments=n)
        dis = jnp.where(deg > 0, jax.lax.rsqrt(deg), 0.0)
        w = -dis[row] * ew * dis[col]

        def prop(h):
            return jax.ops.segment_sum(w[:, None] * h[row], col, num_segments=n)
        tx0 = x
        out = tx0 @ weight[0]
        tx1 = prop(x)
        out = out + tx1 @ weight[1]
        for k in range(2, weight.shape[0]):
            tx2 = 2.0 * prop(tx1) - tx0
            out = out + tx2 @ weight[k]
            tx0, tx1 = (tx1, tx2)
        return out + bias
    edge_index = jnp.stack([src, dst])
    batch0 = jnp.zeros((3125,), jnp.int32)
    x = _layernorm(x + _L0_gnn_ref(x, edge_index, edge_attr_40, edge_weight, node_type_119, node_vec, batch0, L0_gnn_W1, L0_gnn_b1, L0_gnn_W2, L0_gnn_b2, L0_gnn_emb, L0_gnn_adaptW, L0_gnn_gamma, L0_gnn_beta), axis=-1)
    x = _layernorm(x + _L1_gnn_ref(x, edge_index, L1_gnn_weight, L1_gnn_bias), axis=-1)
    return x

_drawn_inputs = setup_inputs


def setup_inputs(seed=0):
    import zlib

    import numpy as np

    out = dict(_drawn_inputs(seed))
    spreads = {'L0_gnn_gamma': (1.0, 0.2), 'L0_gnn_beta': (0.0, 0.1)}
    factors = {'edge_attr_40': 5.791,
     'edge_weight': 4.878,
     'node_vec': 6.257,
     'L0_gnn_W1': 3.373,
     'L0_gnn_b1': 64.0,
     'L0_gnn_W2': 3.22,
     'L0_gnn_b2': 200.0,
     'L0_gnn_emb': 64.0,
     'L0_gnn_adaptW': 64.0,
     'L1_gnn_bias': 8.0}
    for name, (base, spread) in spreads.items():
        noise = np.random.default_rng([zlib.crc32(name.encode()), seed]).standard_normal(out[name].shape)
        drawn = base * np.exp(spread * noise) if base else spread * noise
        out[name] = jnp.asarray(drawn.astype(out[name].dtype))
    for name, factor in factors.items():
        out[name] = (out[name] * factor).astype(out[name].dtype)
    return out
```

```python
from contextlib import ExitStack

import concourse.bass as bass
from concourse import mybir

F32 = mybir.dt.float32
F16 = mybir.dt.float16
BF16 = mybir.dt.bfloat16
I32 = mybir.dt.int32
ALU = mybir.AluOpType
ACT = mybir.ActivationFunctionType
AX = mybir.AxisListType

P = 128
PI = 3.141592653589793
CUTOFF = 6.0
LN_EPS = 1e-5


def gnn_program(nc, x, src, dst, edge_attr, edge_weight, node_type, node_vec, w1t, b1, w2t, b2, embt,
                adaptwt, gamma, beta, cheb_w, cheb_bias, out):
    N, H = x.shape
    E, R = edge_attr.shape
    EMB, NEL = embt.shape
    ORDERS = cheb_w.shape[0]
    NB = -(-N // P)
    LAST = N - (NB - 1) * P
    NPAD = NB * P
    GW = 512
    DG = -(-N // GW)
    BINS = NB * DG
    EP = 125
    NT = E // EP
    BODY = 33
    GT = 3
    GROUPS = BODY // GT
    TURNS = NT // BODY
    LOADS = [(0, 12), (12, 24), (24, 33)]
    assert EP * NT == E and TURNS * BODY == NT
    U = 8
    PAIRS = U // 2
    HALF = U // 2
    TMAX = -(-(-(-E // P) + BINS + NB * U) // U) * U
    TCOLS = -(-TMAX // P)
    REC = H + 4
    CW, SLOC, DSTC, DLOC = H, H + 1, H + 2, H + 3
    SELF = 8192.0
    NTAB = 84
    HM, MULT = EMB, EMB + H
    NCH = NB * H
    CUT = 4 * GW

    rec_dram = nc.dram_tensor("rec_sorted", (TMAX * P, REC), F32).ap()
    node_dram = nc.dram_tensor("node_table", (NPAD, NTAB), F32).ap()
    type_dram = nc.dram_tensor("type_table", (NEL, 2 * EMB), F32).ap()
    hist_dram = nc.dram_tensor("hist_row", (1, BINS), F32).ap()
    bank_dram = nc.dram_tensor("bank_row", (1, P * TCOLS), I32).ap()

    with ExitStack() as ctx:
        def sb(name, shape, dt=F32):
            return ctx.enter_context(nc.sbuf_tensor(name, shape, dt))

        def sem(name):
            return ctx.enter_context(nc.semaphore(name))

        big = sb("big", [P, NB * NPAD // 2])
        counts = big[:, :].bitcast(F16).rearrange("p (b d) -> p b d", b=NB)
        top = [0]

        def part(n):
            top[0] += n
            assert top[0] <= NB * NPAD // 2
            return big[:, top[0] - n:top[0]]

        src_i = part(NT).bitcast(I32)[:EP]
        dst_i = part(NT).bitcast(I32)[:EP]
        tmp_i = part(NT).bitcast(I32)[:EP]
        tmp_j = part(NT).bitcast(I32)[:EP]
        dist = part(NT)[:EP]
        tmp_f = part(NT)[:EP]
        tmp_g = part(NT)[:EP]
        bin_f = part(NT)[:EP]
        aux = part(NT * 4)[:EP].rearrange("p (t f) -> p t f", f=4)
        attr = part(BODY * R)[:EP].rearrange("p (t r) -> p t r", r=R)
        recs = part(BODY * REC)[:EP].rearrange("p (t f) -> p t f", f=REC)
        attr_t = [part(GT * EP)[:R] for _ in range(2)]
        hid = [part(GT * EP)[:H] for _ in range(2)]
        onehot_bin = [part(-(-BINS // 2)).bitcast(F16)[:EP, :BINS] for _ in range(GT)]
        rank_junk = part(BINS)[:EP]
        pos_f = part(BODY)[:EP]
        pos_i = [part(GT).bitcast(I32)[:EP] for _ in range(GROUPS)]
        pad_rec = part(8 * REC)
        iota_bin = part(-(-BINS // 2)).bitcast(F16)[:, :BINS]
        tri_lt = part(P // 2).bitcast(F16)
        tri_ge = part(P // 2).bitcast(F16)
        onehot_sb = part(-(-NB * NT // 2)).bitcast(F16)[:EP, :NB * NT].rearrange("p (b t) -> p b t", b=NB)
        onehot_dg = part(-(-DG * NT // 2)).bitcast(F16)[:EP, :DG * NT].rearrange("p (g t) -> p g t", g=DG)
        bin_starts = part(BINS)
        sb_starts = part(NB)
        tile_ids = part(TCOLS)
        bin_count = part(TCOLS)
        sb_count = part(TCOLS)
        small_junk = part(BINS)
        bank_i = part(TCOLS).bitcast(I32)
        ones_row = part(P)
        hist_sb = part(DG)
        row_f = part(BINS)
        row_i = part(BINS).bitcast(I32)
        row_t = part(BINS)
        row_start = part(BINS)
        sb_tiles = part(NB)
        sb_end = part(NB)
        sb_first = part(NB)
        sb_i = part(NB).bitcast(I32)
        types = part(NB).bitcast(I32)
        iota_i = part(GW).bitcast(I32)
        tile_i = part(TCOLS).bitcast(I32)
        sb_h = part(-(-NT // 2)).bitcast(F16)[:EP, :NT]
        dg_h = part(-(-NT // 2)).bitcast(F16)[:EP, :NT]
        type_rows = part(NB * 2 * EMB).rearrange("p (b f) -> p b f", b=NB)
        nodes = part(NB * NTAB).rearrange("p (b f) -> p b f", b=NB)
        emb_rest = part(NB * EMB).rearrange("p (b e) -> p b e", b=NB)
        type_sb = part(2 * EMB)
        embt_sb = part(NEL)
        adaptwt_sb = part(EMB)

        ident = sb("ident", [P, P])
        ident_h = sb("ident_h", [P, P], F16)
        iota_d = sb("iota_d", [P, GW], F16)
        w1t_sb = sb("w1t_sb", [R, H])
        w2t_sb = sb("w2t_sb", [H, H])
        b1_sb = sb("b1_sb", [H, 1])
        b2_all = sb("b2_all", [P, H])
        gamma_all = sb("gamma_all", [P, H])
        beta_all = sb("beta_all", [P, H])
        bias_all = sb("bias_all", [P, H])
        xs = sb("xs", [P, NB, H])
        mult = sb("mult", [P, NB])
        starts_i = sb("starts_i", [1, NB + 1], I32)
        bank_row = sb("bank_row_sb", [1, P * TCOLS], I32)
        half_pi = sb("half_pi", [P, 1])
        zeros_h = sb("zeros_h", [P, GW], F16)
        cheb_sb = sb("cheb_sb", [2 * H, ORDERS // 2, H])
        agg = sb("agg", [P, NB, H + 1])
        deg2 = sb("deg2", [P, 2, NB])
        dis = sb("dis", [P, NB])
        stat = sb("stat", [P, NB])
        stat_b = sb("stat_b", [P, NB])
        std = sb("std", [P, NB])

        MID = U * (REC + 1 + NTAB + P + P // 2 + GW // 2 + 2 * H + 2) + HALF * P // 2 + 3 * EMB + 3 * NB * EMB // 2
        mid = sb("mid", [P, max(MID, 5 * NCH + 3 * NCH // 2)])
        used = [0]

        def mid_part(n):
            used[0] += n
            return mid[:, used[0] - n:used[0]]

        rin = mid_part(U * REC).rearrange("p (j f) -> p j f", j=U)
        idx = mid_part(U).bitcast(I32)
        ngath = mid_part(U * NTAB).rearrange("p (j f) -> p j f", j=U)
        hot_s = mid_part(U * P).rearrange("p (j s) -> p j s", j=U)
        hot_sh = mid_part(U * P // 2).bitcast(F16).rearrange("p (j s) -> p j s", j=U)
        hot_st = mid_part(HALF * P // 2).bitcast(F16).rearrange("p (j s) -> p j s", j=HALF)
        hot_d = mid_part(U * GW // 2).bitcast(F16).rearrange("p (j s) -> p j s", j=U)
        msg_pre = mid_part(U * H).rearrange("p (j s) -> p j s", j=U)
        msg = mid_part(U * (H + 1)).rearrange("p (j s) -> p j s", j=U)
        adapt = mid_part(U)
        adapt_junk = mid_part(3 * EMB).rearrange("p (s e) -> p s e", s=3)
        emb_parts = mid_part(3 * NB * EMB // 2).bitcast(BF16).rearrange("p (b f) -> p b f", b=NB)
        used[0] = 0

        def node_part(n=NCH):
            return mid_part(n).rearrange("p (b h) -> p b h", b=NB)

        t1, t2, prop, work, square = [node_part() for _ in range(5)]
        parts = mid_part(3 * NCH // 2).bitcast(BF16).rearrange("p (b s h) -> p b s h", b=NB, s=3)
        orders = big[:, :ORDERS * NCH].rearrange("p (b k h) -> p b k h", b=NB, k=ORDERS)
        turned = [big[:2 * H, ORDERS * NCH + j * 2 * P:ORDERS * NCH + (j + 1) * 2 * P].rearrange("p (k n) -> p k n", k=2) for j in range(2)]

        psum = ctx.enter_context(nc.psum_tensor("psum", [P, 8 * GW], F32))

        def bk(b, lo, hi, rows=P):
            return psum[:rows, b * GW + lo:b * GW + hi]

        AGG0 = (DG - 1) * GW + P

        small_loaded = sem("small_loaded")
        edges_loaded = sem("edges_loaded")
        v_step = sem("v_step")
        a_step = sem("a_step")
        g_step = sem("g_step")
        iotas_ready = sem("iotas_ready")
        hots_ready = sem("hots_ready")
        hist_ready = sem("hist_ready")
        hist_copied = sem("hist_copied")
        hist_moved = sem("hist_moved")
        starts_ready = sem("starts_ready")
        bcast_ready = sem("bcast_ready")
        bank_ready = sem("bank_ready")
        bank_moved = sem("bank_moved")
        type_ready = sem("type_ready")
        type_copied = sem("type_copied")
        type_moved = sem("type_moved")
        types_gathered = sem("types_gathered")
        nodes_ready = sem("nodes_ready")
        nodes_moved = sem("nodes_moved")
        angle_ready = sem("angle_ready")
        sine_ready = sem("sine_ready")
        pad_ready = sem("pad_ready")
        attr_loaded = [sem(f"attr_loaded{s}") for s in range(len(LOADS))]
        attr_turned = sem("attr_turned")
        attr_copied = sem("attr_copied")
        hid_ready = sem("hid_ready")
        silu_done = sem("silu_done")
        gate_ready = sem("gate_ready")
        gate_copied = sem("gate_copied")
        bin_hot = sem("bin_hot")
        rank_ready = sem("rank_ready")
        rank_read = sem("rank_read")
        rank_added = sem("rank_added")
        record_ready = sem("record_ready")
        pool_tick = sem("pool_tick")
        scattered = [sem(f"scattered{g}") for g in range(GROUPS)]
        rec_loaded = [sem(f"rec_loaded{s}") for s in range(PAIRS)]
        idx_ready = sem("idx_ready")
        gathered = [sem(f"gathered{j}") for j in range(U)]
        hot_ready = sem("hot_ready")
        hot_turned = sem("hot_turned")
        hot_copied = sem("hot_copied")
        emb_ready = sem("emb_ready")
        adapt_done = sem("adapt_done")
        pre_ready = sem("pre_ready")
        msg_ready = sem("msg_ready")
        summed = sem("summed")
        row_stored_v = sem("row_stored_v")
        row_stored_a = sem("row_stored_a")
        agg_stored = sem("agg_stored")
        var_ready = sem("var_ready")
        std_ready = sem("std_ready")
        split_ready = sem("split_ready")
        prop_ready = sem("prop_ready")
        prop_read = sem("prop_read")
        turn_ready = sem("turn_ready")
        turn_copied = sem("turn_copied")
        proj_ready = sem("proj_ready")
        orders_copied = sem("orders_copied")
        act_tick = sem("act_tick")
        pe_tick = sem("pe_tick")
        v_tick = sem("v_tick")
        orders_ready = sem("orders_ready")
        out_ready = sem("out_ready")
        stored = sem("stored")

        def row_of(v):
            return v.rearrange("(a n) -> a n", a=1)

        xb = x[:(NB - 1) * P].rearrange("(b p) h -> p b h", p=P)
        outb = out[:(NB - 1) * P].rearrange("(b p) h -> p b h", p=P)
        SMALL = 9 + ORDERS // 2 + 6

        block = ctx.enter_context(nc.Block())

        @block.sync
        def _(sp):
            sp.dma_start(src_i, src.rearrange("(p t) -> p t", p=EP)).then_inc(edges_loaded, 16)
            sp.dma_start(dst_i, dst.rearrange("(p t) -> p t", p=EP)).then_inc(edges_loaded, 16)
            sp.dma_start(dist, edge_weight.rearrange("(p t) -> p t", p=EP)).then_inc(edges_loaded, 16)
            sp.dma_start(embt_sb[:EMB], embt).then_inc(small_loaded, 16)
            sp.dma_start(adaptwt_sb[:EMB], adaptwt).then_inc(small_loaded, 16)
            sp.dma_start(w1t_sb[:, :], w1t).then_inc(small_loaded, 16)
            sp.dma_start(w2t_sb[:, :], w2t).then_inc(small_loaded, 16)
            sp.dma_start(b1_sb[:, :], b1.rearrange("(h a) -> h a", a=1)).then_inc(small_loaded, 16)
            sp.dma_start(b2_all[:, :], row_of(b2).to_broadcast([P, H])).then_inc(small_loaded, 16)
            sp.dma_start(gamma_all[:, :], row_of(gamma).to_broadcast([P, H])).then_inc(small_loaded, 16)
            sp.dma_start(beta_all[:, :], row_of(beta).to_broadcast([P, H])).then_inc(small_loaded, 16)
            sp.dma_start(bias_all[:, :], row_of(cheb_bias).to_broadcast([P, H])).then_inc(small_loaded, 16)
            for k in range(ORDERS // 2):
                sp.dma_start(cheb_sb[:, k, :], cheb_w[2 * k:2 * k + 2].rearrange("k i o -> (k i) o")).then_inc(small_loaded, 16)
            sp.wait_ge(pad_ready, 1)
            sp.dma_start(xs[:, :NB - 1, :], xb).then_inc(small_loaded, 16)
            sp.dma_start(xs[:LAST, NB - 1, :], x[(NB - 1) * P:]).then_inc(small_loaded, 16)
            sp.dma_start(mult[:, :NB - 1], node_vec[:(NB - 1) * P].rearrange("(b p) -> p b", p=P),
                         allow_slow_non_contiguous=True).then_inc(small_loaded, 16)
            sp.dma_start(mult[:LAST, NB - 1:NB], node_vec[(NB - 1) * P:].rearrange("(p a) -> p a", a=1)).then_inc(small_loaded, 16)
            sp.dma_start(types[:, :NB - 1], node_type[:(NB - 1) * P].rearrange("(b p) -> p b", p=P),
                         allow_slow_non_contiguous=True).then_inc(small_loaded, 16)
            sp.dma_start(types[:LAST, NB - 1:NB], node_type[(NB - 1) * P:].rearrange("(p a) -> p a", a=1)).then_inc(small_loaded, 16)
            for s, (lo, hi) in enumerate(LOADS):
                sp.dma_start(attr[:, lo:hi, :], edge_attr.rearrange("(p t) r -> p t r", p=EP)[:, lo:hi, :]).then_inc(attr_loaded[s], 16)
            sp.wait_ge(type_copied, 1)
            sp.dma_start(type_dram, type_sb[:NEL]).then_inc(type_moved, 16)
            sp.wait_ge(hist_copied, 1)
            sp.dma_start(hist_dram.rearrange("a (b g) -> (a b) g", b=NB), hist_sb[:NB]).then_inc(hist_moved, 16)
            sp.wait_ge(hist_moved, 16)
            sp.dma_start(row_f[:1], hist_dram).then_inc(hist_moved, 16)
            sp.wait_ge(bank_ready, 1)
            sp.dma_start(bank_dram.rearrange("a (p c) -> (a p) c", p=P), bank_i).then_inc(bank_moved, 16)
            sp.wait_ge(bank_moved, 16)
            sp.dma_start(bank_row[:, :], bank_dram).then_inc(bank_moved, 16)
            sp.wait_ge(nodes_ready, 1)
            sp.dma_start(node_dram.rearrange("(b p) f -> p b f", p=P), nodes[:, :, :]).then_inc(nodes_moved, 16)
            ea = edge_attr.rearrange("(p t) r -> p t r", p=EP)
            with sp.Fori(1, TURNS) as i:
                for s, (lo, hi) in enumerate(LOADS):
                    sp.wait_ge(attr_turned, (i - 1) * GROUPS + hi // GT)
                    sp.dma_start(attr[:, lo:hi, :], ea[:, bass.ds(i * BODY + lo, hi - lo), :]).then_inc(attr_loaded[s], 16)
            for g in range(GROUPS):
                sp.wait_ge(scattered[g], 16 + 16 * GT * TURNS)
            turns = sp.value_load(starts_i[0:1, NB:NB + 1], min_val=1, max_val=TMAX // U)
            rd = rec_dram.rearrange("(q j p) f -> p q j f", p=P, j=2)
            with sp.Fori(0, turns) as q:
                for s in range(PAIRS):
                    sp.wait_ge(msg_ready, q * U + 2 * s + 2)
                    sp.dma_start(rin[:, 2 * s:2 * s + 2, :], rd[:, bass.ds(q * PAIRS + s, 1), :, :].rearrange("p q j f -> p (q j) f")).then_inc(rec_loaded[s], 16)
            sp.wait_ge(out_ready, 1)
            sp.dma_start(outb, xs[:, :NB - 1, :]).then_inc(stored, 16)
            sp.dma_start(out[(NB - 1) * P:], xs[:LAST, NB - 1, :]).then_inc(stored, 16)
            sp.wait_ge(stored, 32)

        @block.gpsimd
        def _(gp):
            n = 0

            def then_wait(inst):
                nonlocal n
                n += 1
                inst.then_inc(g_step, 1)
                gp.wait_ge(g_step, n)

            then_wait(gp.memset(xs[:, NB - 1, :], 0.0))
            then_wait(gp.memset(mult[:, NB - 1:NB], 0.0))
            then_wait(gp.memset(types[:, NB - 1:NB], 0))
            then_wait(gp.memset(pad_rec, 0.0))
            padv = pad_rec.rearrange("p (k f) -> p k f", f=REC)
            then_wait(gp.memset(padv[:, :, SLOC], -1.0))
            then_wait(gp.memset(padv[:, :, DLOC], SELF))
            gp.sem_inc(pad_ready, 1)
            for g in range(GROUPS):
                lo, hi = TMAX // 8 * g // GROUPS * 8, TMAX // 8 * (g + 1) // GROUPS * 8
                gp.dma_start(rec_dram[lo * P:hi * P].rearrange("(c p k) f -> p c (k f)", p=P, k=8),
                             pad_rec.unsqueeze(1).to_broadcast([P, (hi - lo) // 8, 8 * REC])).then_inc(scattered[g], 16)
            then_wait(gp.iota(iota_i, [[1, GW]], base=0, channel_multiplier=0))
            then_wait(gp.tensor_copy(iota_d[:, :], iota_i))
            then_wait(gp.tensor_copy(iota_bin, iota_i[:, :BINS]))
            then_wait(gp.iota(tile_i, [[1, TCOLS]], base=0, channel_multiplier=TCOLS))
            then_wait(gp.tensor_copy(tile_ids, tile_i))
            then_wait(gp.memset(zeros_h[:, :], 0.0))
            then_wait(gp.memset(ones_row, 1.0))
            then_wait(gp.memset(nodes[:, :, MULT + 1:], 0.0))
            then_wait(gp.memset(half_pi[:, :], PI / 2))
            then_wait(gp.memset(tri_ge, 1.0))
            then_wait(gp.affine_select(tri_lt, tri_ge, [[1, P]], ALU.is_gt, 0.0, base=0, channel_multiplier=-1))
            then_wait(gp.affine_select(tri_ge, tri_ge, [[-1, P]], ALU.is_ge, 0.0, base=0, channel_multiplier=1))
            then_wait(gp.memset(ident[:, :], 1.0))
            then_wait(gp.affine_select(ident[:, :], ident[:, :], [[1, P]], ALU.is_equal, 0.0, base=0, channel_multiplier=-1))
            then_wait(gp.tensor_copy(ident_h[:, :], ident[:, :]))
            gp.sem_inc(iotas_ready, 1)
            gp.wait_ge(small_loaded, SMALL * 16)
            gp.wait_ge(type_moved, 16)
            for b in range(NB):
                gp.indirect_dma_start(type_rows[:, b, :], None, type_dram, bass.IndirectOffsetOnAxis(ap=types[:, b:b + 1], axis=0)).then_inc(types_gathered, 16)
            for g in range(GROUPS):
                gp.wait_ge(scattered[g], 16)
            with gp.Fori(0, TURNS) as i:
                for g in range(GROUPS):
                    gp.wait_ge(record_ready, i * (3 * GROUPS) + 3 * (g + 1))
                    gp.sem_inc(pool_tick, 1)
                    for k in range(GT):
                        gp.indirect_dma_start(rec_dram, bass.IndirectOffsetOnAxis(ap=pos_i[g][:, k:k + 1], axis=0),
                                              recs[:, g * GT + k, :], None).then_inc(scattered[g], 16)
            gp.wait_ge(nodes_moved, 16)
            gp.wait_ge(starts_ready, 1)
            last = gp.value_load(starts_i[0:1, NB:NB + 1], min_val=1, max_val=TMAX // U)
            with gp.Fori(0, last) as q:
                for s in range(PAIRS):
                    gp.wait_ge(rec_loaded[s], q * 16 + 16)
                    gp.sem_inc(pool_tick, 1)
                    gp.wait_ge(msg_ready, q * U + 2 * s + 2)
                    gp.sem_inc(pool_tick, 1)
                    gp.tensor_copy(idx[:, 2 * s:2 * s + 2], rin[:, 2 * s:2 * s + 2, DSTC]).then_inc(idx_ready, 1)
                    gp.wait_ge(idx_ready, q * PAIRS + s + 1)
                    gp.sem_inc(pool_tick, 1)
                    for j in (2 * s, 2 * s + 1):
                        gp.indirect_dma_start(ngath[:, j, :], None, node_dram, bass.IndirectOffsetOnAxis(ap=idx[:, j:j + 1], axis=0)).then_inc(gathered[j], 16)

        @block.scalar
        def _(act):
            n = 0

            def then_wait(inst):
                nonlocal n
                n += 1
                inst.then_inc(a_step, 1)
                act.wait_ge(a_step, n)

            act.sem_inc(attr_copied, 1)
            act.sem_inc(silu_done, 1)
            act.sem_inc(msg_ready, U)
            act.wait_ge(iotas_ready, 1)
            act.wait_ge(angle_ready, 1)
            act.activation(tmp_g, tmp_f, ACT.Sin, bias=half_pi[:EP, :], scale=-PI / CUTOFF).then_inc(sine_ready, 1)
            act.wait_ge(type_ready, 1)
            then_wait(act.copy(type_sb[:NEL], bk(0, 0, 2 * EMB, NEL)))
            act.sem_inc(type_copied, 1)
            act.wait_ge(small_loaded, SMALL * 16)
            with act.Fori(0, TURNS) as i:
                for g in range(GROUPS):
                    act.wait_ge(attr_turned, i * GROUPS + g + 1)
                    act.wait_ge(hid_ready, i * GROUPS + max(g - 1, 0) + 1)
                    act.copy(attr_t[g % 2], bk(g % 2, 0, GT * EP, R)).then_inc(attr_copied, 1)
                    act.wait_ge(hid_ready, i * GROUPS + g + 2)
                    act.wait_ge(gate_ready, i * GROUPS + max(g - 1, 0) + 1)
                    act.activation(hid[g % 2], bk(2 + g % 2, 0, GT * EP, H), ACT.Silu, bias=b1_sb[:, :]).then_inc(silu_done, 1)
            act.sem_inc(row_stored_a, 1)
            act.wait_ge(starts_ready, 1)
            with act.Fori(0, NB) as b:
                q0 = act.value_load(starts_i[0:1, bass.ds(b, 1)], min_val=0, max_val=TMAX // U - 1)
                q1 = act.value_load(starts_i[0:1, bass.ds(b + 1, 1)], min_val=1, max_val=TMAX // U)
                with act.Fori(q0, q1) as q:
                    for h in range(2):
                        act.wait_ge(hot_turned, q * 2 + h + 1)
                        act.sem_inc(act_tick, 1)
                        act.wait_ge(emb_ready, q * 2 + h + 1)
                        act.copy(hot_st, bk(7, 0, HALF * P // 2).bitcast(F16).rearrange("p (j s) -> p j s", j=HALF)).then_inc(hot_copied, 1)
                        js = range(h * HALF, (h + 1) * HALF)
                        act.wait_ge(pre_ready, q * U + js[-1] + 1)
                        act.copy(msg[:, js[0]:js[-1] + 1, H], ngath[:, js[0]:js[-1] + 1, MULT])
                        for j in js:
                            act.activation(msg[:, j, :H], msg_pre[:, j, :], ACT.Copy, scale=rin[:, j, CW:CW + 1]).then_inc(msg_ready, 1)
                act.wait_ge(summed, q1 * U + U)
                act.sem_inc(act_tick, 1)
                act.activation(counts[:, bass.ds(b, 1), :CUT].rearrange("p b d -> p (b d)"), psum[:, :CUT], ACT.Copy, scale=0.5,
                               accum_out=deg2[:, 0, bass.ds(b, 1)]).then_inc(row_stored_a, 1)
            for k in range(3):
                act.wait_ge(var_ready, k + 1)
                act.activation(std[:, :], stat[:, :], ACT.Sqrt).then_inc(std_ready, 1)
            act.wait_ge(orders_ready, 1)
            for k, t in enumerate((xs[:, :, :], t1, t2)):
                act.copy(orders[:, :, k, :], t).then_inc(orders_copied, 1)
            for b in range(NB):
                act.wait_ge(turn_ready, b + 1)
                if b >= 2:
                    act.wait_ge(proj_ready, b - 1)
                act.copy(turned[b % 2], bk(5 + b % 2, 0, 2 * P, 2 * H).rearrange("p (k n) -> p k n", k=2)).then_inc(turn_copied, 1)
            act.wait_ge(var_ready, 4)
            act.activation(std[:, :], stat[:, :], ACT.Sqrt).then_inc(std_ready, 1)

        @block.tensor
        def _(pe):
            pe.sem_inc(hid_ready, 1)
            pe.sem_inc(gate_ready, 1)
            pe.sem_inc(rank_added, GT)
            pe.sem_inc(emb_ready, 1)
            pe.sem_inc(summed, U)
            pe.wait_ge(iotas_ready, 1)
            pe.wait_ge(small_loaded, SMALL * 16)
            pe.matmul(bk(0, 0, EMB, NEL), embt_sb[:EMB], adaptwt_sb[:EMB], start=True, stop=True)
            pe.transpose(bk(0, EMB, 2 * EMB, NEL), embt_sb[:EMB], ident[:EMB, :EMB]).then_inc(type_ready, 1)
            pe.wait_ge(hots_ready, 1)
            pe.matmul(bk(1, 0, DG), zeros_h[:, :P], zeros_h[:, :DG], start=True, stop=False, skip_group_check=True)
            with pe.Fori(0, TURNS) as i:
                for j in range(BODY):
                    pe.matmul(bk(1, 0, DG, NB), onehot_sb[:, :, bass.ds(i * BODY + j, 1)].rearrange("p b t -> p (b t)"),
                              onehot_dg[:, :, bass.ds(i * BODY + j, 1)].rearrange("p b t -> p (b t)"), start=False, stop=False, skip_group_check=True)
            pe.matmul(bk(1, 0, DG), zeros_h[:, :P], zeros_h[:, :DG], start=False, stop=True, skip_group_check=True).then_inc(hist_ready, 1)
            pe.wait_ge(starts_ready, 1)
            pe.matmul(bk(0, 0, BINS), ones_row[:1], row_start[:1], start=True, stop=True)
            pe.matmul(bk(0, BINS, BINS + NB), ones_row[:1], sb_first[:1], start=True, stop=True).then_inc(bcast_ready, 1)
            pe.matmul(bk(6, 0, BINS, EP), ones_row[:1, :EP], row_f[:1], start=True, stop=False, skip_group_check=True)

            with pe.Fori(0, TURNS) as i:
                def earlier(t):
                    pe.wait_ge(bin_hot, i * BODY + t + 1)
                    pe.matmul(bk(6, 0, BINS, EP), tri_lt[:EP, :EP], onehot_bin[t % GT], start=False, stop=False, skip_group_check=True).then_inc(rank_ready, 1)

                def others(t):
                    pe.wait_ge(rank_read, i * BODY + t + 1)
                    pe.matmul(bk(6, 0, BINS, EP), tri_ge[:EP, :EP], onehot_bin[t % GT], start=False, stop=False, skip_group_check=True).then_inc(rank_added, 1)

                for g in range(GROUPS):
                    earlier(g * GT)
                    for s, (lo, hi) in enumerate(LOADS):
                        if g * GT == lo:
                            pe.wait_ge(attr_loaded[s], i * 16 + 16)
                    pe.wait_ge(attr_copied, i * GROUPS + max(g - 1, 0) + 1)
                    pe.sem_inc(pe_tick, 1)
                    for k in range(GT):
                        mm = pe.transpose(bk(g % 2, k * EP, (k + 1) * EP, R), attr[:, g * GT + k, :], ident[:EP, :EP])
                    mm.then_inc(attr_turned, 1)
                    others(g * GT)
                    earlier(g * GT + 1)
                    pe.wait_ge(attr_copied, i * GROUPS + g + 2)
                    pe.wait_ge(silu_done, i * GROUPS + max(g - 1, 0) + 1)
                    pe.sem_inc(pe_tick, 1)
                    pe.matmul(bk(2 + g % 2, 0, GT * EP, H), w1t_sb[:, :], attr_t[g % 2], start=True, stop=True).then_inc(hid_ready, 1)
                    others(g * GT + 1)
                    earlier(g * GT + 2)
                    pe.wait_ge(silu_done, i * GROUPS + g + 2)
                    pe.wait_ge(gate_copied, i * GROUPS + max(g - 1, 0) + 1)
                    for k in range(GT):
                        mm = pe.matmul(bk(4 + g % 2, k * H, (k + 1) * H, EP), hid[g % 2][:, k * EP:(k + 1) * EP], w2t_sb[:, :], start=True, stop=True)
                    mm.then_inc(gate_ready, 1)
                    others(g * GT + 2)

            pe.wait_ge(bank_moved, 32)
            with pe.Fori(0, NB) as b:
                q0 = pe.value_load(starts_i[0:1, bass.ds(b, 1)], min_val=0, max_val=TMAX // U - 1)
                q1 = pe.value_load(starts_i[0:1, bass.ds(b + 1, 1)], min_val=1, max_val=TMAX // U)
                pe.wait_ge(row_stored_v, b + 1)
                pe.wait_ge(row_stored_a, b + 1)
                for g in range(DG):
                    pe.matmul(bk(g, 0, GW), zeros_h[:, :P], zeros_h[:, :], start=True, stop=False, skip_group_check=True)
                with pe.Fori(q0, q1) as q:
                    def turn(h):
                        pe.wait_ge(hot_ready, q * U + (h + 1) * HALF)
                        pe.sem_inc(pe_tick, 1)
                        pe.wait_ge(adapt_done, q * U + h * HALF + HALF)
                        for k in range(HALF):
                            mm = pe.transpose(bk(7, k * P // 2, (k + 1) * P // 2).bitcast(F16), hot_sh[:, h * HALF + k, :], ident_h[:, :])
                        mm.then_inc(hot_turned, 1)

                    def count(h):
                        for j in range(h * HALF, (h + 1) * HALF):
                            column = pe.value_load(bank_row[0:1, bass.ds(q * U + j, 1)], min_val=0, max_val=(DG - 1) * GW)
                            pe.wait_ge(hot_ready, q * U + j + 1)
                            pe.matmul(psum[:, bass.ds(column, GW)], hot_sh[:, j, :], hot_d[:, j, :], start=False, stop=False, skip_group_check=True)

                    def embed(h):
                        pe.wait_ge(hot_copied, q * 2 + h + 1)
                        for k in range(HALF):
                            mm = pe.matmul(bk(7, k * 3 * EMB, (k + 1) * 3 * EMB), hot_st[:, k, :],
                                           emb_parts[:, bass.ds(b, 1), :].rearrange("p b e -> p (b e)"), start=True, stop=True)
                        mm.then_inc(emb_ready, 1)

                    def add_messages(h):
                        for j in range(h * HALF, (h + 1) * HALF):
                            pe.wait_ge(msg_ready, q * U + j + 1 + U)
                            pe.matmul(psum[:, AGG0:AGG0 + H + 1], hot_s[:, j, :], msg[:, j, :], start=False, stop=False, skip_group_check=True).then_inc(summed, 1)

                    turn(0)
                    count(0)
                    embed(0)
                    count(1)
                    turn(1)
                    add_messages(0)
                    embed(1)
                    add_messages(1)

            pe.wait_ge(row_stored_v, NB + 1)
            pe.wait_ge(row_stored_a, NB + 1)
            for k in range(1, ORDERS):
                pe.wait_ge(split_ready, k)
                with pe.Fori(0, NB // 5) as i:
                    for j in range(5):
                        pe.wait_ge(prop_read, i * 5 + (k - 1) * NB + j + 1)
                        for s in range(NB):
                            mm = pe.matmul(bk(j, 0, 3 * H), counts[:, s, bass.ds((i * 5 + j) * P, P)], parts[:, s, :, :].rearrange("p s h -> p (s h)"), start=(s == 0), stop=(s == NB - 1))
                        mm.then_inc(prop_ready, 1)
            pe.wait_ge(orders_ready, 1)
            pe.wait_ge(orders_copied, 3)
            for b in range(NB):
                if b >= 2:
                    pe.wait_ge(turn_copied, b - 1)
                for k in range(2):
                    mm = pe.transpose(bk(5 + b % 2, k * P, (k + 1) * P, 2 * H), orders[:, b, 2 * k:2 * k + 2, :].rearrange("p k h -> p (k h)"), ident[:, :])
                mm.then_inc(turn_ready, 1)
                pe.wait_ge(turn_copied, b + 1)
                o = b % 9 * H
                pe.matmul(bk(b // 9, o, o + H), turned[b % 2][:, 0, :], cheb_sb[:, 0, :], start=True, stop=False)
                pe.matmul(bk(b // 9, o, o + H), turned[b % 2][:, 1, :], cheb_sb[:, 1, :], start=False, stop=True).then_inc(proj_ready, 1)

        @block.vector
        def _(v):
            n = 0

            def then_wait(inst):
                nonlocal n
                n += 1
                inst.then_inc(v_step, 1)
                v.wait_ge(v_step, n)

            v.sem_inc(gate_copied, 1)
            v.sem_inc(adapt_done, HALF)
            v.sem_inc(prop_read, 5)
            v.wait_ge(edges_loaded, 3 * 16)
            then_wait(v.tensor_scalar(tmp_i, src_i, 7, None, ALU.logical_shift_right))
            then_wait(v.tensor_scalar(tmp_j, dst_i, 9, None, ALU.logical_shift_right))
            then_wait(v.tensor_copy(sb_h, tmp_i))
            then_wait(v.tensor_copy(dg_h, tmp_j))
            for b in range(NB):
                v.tensor_scalar(onehot_sb[:, b, :], sb_h, float(b), None, ALU.is_equal)
            for g in range(DG - 1):
                v.tensor_scalar(onehot_dg[:, g, :], dg_h, float(g), None, ALU.is_equal)
            then_wait(v.tensor_scalar(onehot_dg[:, DG - 1, :], dg_h, float(DG - 1), None, ALU.is_equal))
            v.sem_inc(hots_ready, 1)
            then_wait(v.scalar_tensor_tensor(out=bin_f, in0=tmp_i, scalar=float(DG), in1=tmp_j, op0=ALU.mult, op1=ALU.add))
            then_wait(v.scalar_tensor_tensor(out=tmp_g, in0=dist, scalar=-1.0, in1=dist, op0=ALU.mult, op1=ALU.max))
            then_wait(v.tensor_scalar(tmp_i, tmp_g, 1.0 / (2 * CUTOFF), None, ALU.mult))
            then_wait(v.scalar_tensor_tensor(out=tmp_f, in0=tmp_i, scalar=-2 * CUTOFF, in1=tmp_g, op0=ALU.mult, op1=ALU.add))
            then_wait(v.scalar_tensor_tensor(out=tmp_f, in0=tmp_f, scalar=-1.0, in1=tmp_f, op0=ALU.mult, op1=ALU.max))
            then_wait(v.tensor_scalar(tmp_g, tmp_f, -1.0, 2 * CUTOFF, ALU.mult, ALU.add))
            then_wait(v.tensor_tensor(tmp_f, tmp_f, tmp_g, ALU.min))
            v.sem_inc(angle_ready, 1)
            then_wait(v.tensor_scalar(tmp_j, src_i, P - 1, None, ALU.bitwise_and))
            then_wait(v.tensor_copy(aux[:, :, 1], tmp_j))
            then_wait(v.tensor_copy(aux[:, :, 2], dst_i))
            then_wait(v.tensor_tensor(tmp_i, src_i, dst_i, ALU.is_equal))
            then_wait(v.tensor_scalar(tmp_j, dst_i, GW - 1, None, ALU.bitwise_and))
            then_wait(v.scalar_tensor_tensor(out=aux[:, :, 3], in0=tmp_i, scalar=SELF, in1=tmp_j, op0=ALU.mult, op1=ALU.add))
            v.wait_ge(sine_ready, 1)
            then_wait(v.tensor_scalar(tmp_g, tmp_g, 0.5, 0.5, ALU.mult, ALU.add))
            then_wait(v.scalar_tensor_tensor(out=aux[:, :, 0], in0=dist, scalar=CUTOFF, in1=tmp_g, op0=ALU.is_lt, op1=ALU.mult))
            v.wait_ge(iotas_ready, 1)
            v.wait_ge(hist_ready, 1)
            then_wait(v.tensor_copy(hist_sb[:NB], bk(1, 0, DG, NB)))
            v.sem_inc(hist_copied, 1)
            v.wait_ge(hist_moved, 32)
            then_wait(v.tensor_scalar(row_i[:1], row_f[:1], P - 1.0, None, ALU.add))
            then_wait(v.tensor_scalar(row_i[:1], row_i[:1], 7, None, ALU.logical_shift_right))
            then_wait(v.tensor_copy(row_t[:1], row_i[:1]))
            tiles = row_t[:1].rearrange("a (b g) -> a b g", b=NB)
            start = row_start[:1].rearrange("a (b g) -> a b g", b=NB)
            then_wait(v.tensor_reduce(sb_tiles[:1], tiles, AX.X, ALU.add))
            then_wait(v.tensor_scalar(sb_i[:1], sb_tiles[:1], U - 1.0, float(U), ALU.add, ALU.max))
            then_wait(v.tensor_scalar(sb_i[:1], sb_i[:1], U.bit_length() - 1, None, ALU.logical_shift_right))
            then_wait(v.tensor_copy(sb_tiles[:1], sb_i[:1]))
            then_wait(v.tensor_tensor_scan(sb_end[:1], ones_row[:1, :NB], sb_tiles[:1], 0.0, ALU.mult, ALU.add))
            then_wait(v.tensor_tensor(sb_first[:1], sb_end[:1], sb_tiles[:1], ALU.subtract))
            then_wait(v.tensor_copy(starts_i[:, :NB], sb_first[:1]))
            then_wait(v.tensor_copy(starts_i[:, NB:], sb_end[:1, NB - 1:]))
            then_wait(v.tensor_scalar(sb_first[:1], sb_first[:1], float(U), None, ALU.mult))
            then_wait(v.tensor_copy(start[:, :, 0], sb_first[:1]))
            for g in range(1, DG):
                then_wait(v.tensor_tensor(start[:, :, g], start[:, :, g - 1], tiles[:, :, g - 1], ALU.add))
            then_wait(v.tensor_scalar(row_f[:1], row_start[:1], float(P), None, ALU.mult))
            v.sem_inc(starts_ready, 1)
            v.wait_ge(bcast_ready, 1)
            then_wait(v.tensor_copy(bin_starts, bk(0, 0, BINS)))
            then_wait(v.tensor_copy(sb_starts, bk(0, BINS, BINS + NB)))
            for c in range(TCOLS):
                then_wait(v.tensor_scalar(small_junk, bin_starts, tile_ids[:, c:c + 1], None, ALU.is_le))
                then_wait(v.tensor_reduce(bin_count[:, c:c + 1], small_junk, AX.X, ALU.add))
                then_wait(v.tensor_scalar(small_junk[:, :NB], sb_starts, tile_ids[:, c:c + 1], None, ALU.is_le))
                then_wait(v.tensor_reduce(sb_count[:, c:c + 1], small_junk[:, :NB], AX.X, ALU.add))
            then_wait(v.tensor_scalar(bin_count, bin_count, float(GW), float(GW * (DG - 1)), ALU.mult, ALU.add))
            then_wait(v.scalar_tensor_tensor(out=bank_i, in0=sb_count, scalar=-float(GW * DG), in1=bin_count, op0=ALU.mult, op1=ALU.add))
            v.sem_inc(bank_ready, 1)
            v.wait_ge(small_loaded, SMALL * 16)
            v.wait_ge(types_gathered, NB * 16)
            then_wait(v.tensor_copy(nodes[:, :, :EMB], type_rows[:, :, :EMB]))
            then_wait(v.tensor_copy(emb_rest, type_rows[:, :, EMB:]))
            for k in range(3):
                then_wait(v.tensor_copy(emb_parts[:, :, k * EMB:(k + 1) * EMB], emb_rest))
                if k < 2:
                    then_wait(v.tensor_tensor(emb_rest, emb_rest, emb_parts[:, :, k * EMB:(k + 1) * EMB], ALU.subtract))
            then_wait(v.tensor_tensor(nodes[:, :, HM:HM + H], xs[:, :, :], mult[:, :].unsqueeze(2).to_broadcast([P, NB, H]), ALU.mult))
            then_wait(v.tensor_copy(nodes[:, :, MULT], mult[:, :]))
            v.sem_inc(nodes_ready, 1)

            with v.Fori(0, TURNS) as i:
                for g in range(GROUPS):
                    for k in range(GT):
                        t = g * GT + k
                        v.wait_ge(rank_added, i * BODY + t + 1)
                        v.tensor_scalar(onehot_bin[k], iota_bin[:EP], bin_f[:, bass.ds(i * BODY + t, 1)], None, ALU.is_equal).then_inc(bin_hot, 1)
                    for k in range(GT):
                        t = g * GT + k
                        v.wait_ge(rank_ready, i * BODY + t + 1)
                        v.tensor_tensor_reduce(rank_junk, bk(6, 0, BINS, EP), onehot_bin[k], 1.0, 0.0, ALU.mult, ALU.add, pos_f[:, t:t + 1]).then_inc(rank_read, 1)
                    v.wait_ge(scattered[g], i * (16 * GT) + 16)
                    v.sem_inc(v_tick, 1)
                    v.wait_ge(rank_read, i * BODY + g * GT + GT)
                    v.tensor_copy(pos_i[g], pos_f[:, g * GT:(g + 1) * GT]).then_inc(record_ready, 1)
                    v.tensor_copy(recs[:, g * GT:(g + 1) * GT, H:], aux[:, bass.ds(i * BODY + g * GT, GT), :]).then_inc(record_ready, 1)
                    v.wait_ge(gate_ready, i * GROUPS + g + 2)
                    v.tensor_tensor(recs[:, g * GT:(g + 1) * GT, :H], bk(4 + g % 2, 0, GT * H, EP).rearrange("p (k h) -> p k h", k=GT),
                                    b2_all[:EP, :].unsqueeze(1).to_broadcast([EP, GT, H]), ALU.add).then_inc(gate_copied, 1)
                    v.wait_ge(gate_copied, i * GROUPS + g + 2)
                    v.sem_inc(record_ready, 1)
            v.sem_inc(row_stored_v, 1)

            with v.Fori(0, NB) as b:
                q0 = v.value_load(starts_i[0:1, bass.ds(b, 1)], min_val=0, max_val=TMAX // U - 1)
                q1 = v.value_load(starts_i[0:1, bass.ds(b + 1, 1)], min_val=1, max_val=TMAX // U)
                with v.Fori(q0, q1) as q:
                    def hots(h):
                        v.wait_ge(summed, q * U + (h + 1) * HALF)
                        v.sem_inc(v_tick, 1)
                        for j in range(h * HALF, (h + 1) * HALF):
                            if j % 2 == 0:
                                v.wait_ge(rec_loaded[j // 2], q * 16 + 16)
                            v.tensor_scalar(hot_s[:, j, :], iota_d[:, :P], rin[:, j, SLOC:SLOC + 1], None, ALU.is_equal)
                            v.tensor_scalar(hot_sh[:, j, :], iota_d[:, :P], rin[:, j, SLOC:SLOC + 1], None, ALU.is_equal)
                            v.tensor_scalar(hot_d[:, j, :], iota_d[:, :], rin[:, j, DLOC:DLOC + 1], None, ALU.is_equal).then_inc(hot_ready, 1)

                    def messages(h):
                        v.wait_ge(emb_ready, q * 2 + h + 2)
                        v.sem_inc(v_tick, 1)
                        for j in range(h * HALF, (h + 1) * HALF):
                            k = j % HALF
                            v.wait_ge(gathered[j], q * 16 + 16)
                            if j:
                                v.sem_inc(v_tick, 1)
                                v.wait_ge(adapt_done, q * U + j + HALF)
                            v.tensor_tensor_reduce(adapt_junk, bk(7, k * 3 * EMB, (k + 1) * 3 * EMB).rearrange("p (s e) -> p s e", s=3),
                                                   ngath[:, j, :EMB].unsqueeze(1).to_broadcast([P, 3, EMB]), 1.0, 0.0,
                                                   ALU.mult, ALU.add, adapt[:, j:j + 1]).then_inc(adapt_done, 1)
                        for j in range(h * HALF, (h + 1) * HALF):
                            v.wait_ge(adapt_done, q * U + j + 1 + HALF)
                            v.scalar_tensor_tensor(out=msg_pre[:, j, :], in0=rin[:, j, :H], scalar=adapt[:, j:j + 1],
                                                   in1=ngath[:, j, HM:HM + H], op0=ALU.add, op1=ALU.mult).then_inc(pre_ready, 1)

                    hots(0)
                    hots(1)
                    messages(0)
                    messages(1)
                v.wait_ge(summed, q1 * U + U)
                v.sem_inc(v_tick, 1)
                v.tensor_scalar(counts[:, bass.ds(b, 1), CUT:].rearrange("p b d -> p (b d)"), psum[:, CUT:NPAD], 0.5, None, ALU.mult, ALU.add,
                                accum_out=deg2[:, 1, bass.ds(b, 1)])
                v.tensor_copy(agg[:, bass.ds(b, 1), :].rearrange("p b h -> p (b h)"), psum[:, AGG0:AGG0 + H + 1]).then_inc(row_stored_v, 1)

            def bc(a):
                return a.unsqueeze(2).to_broadcast([P, NB, H])

            def all_blocks(a):
                return a[:, :].unsqueeze(1).to_broadcast([P, NB, H])

            roots = 0

            def root():
                nonlocal roots
                roots += 1
                v.sem_inc(var_ready, 1)
                v.wait_ge(std_ready, roots)

            def norm(dst_t, src_t):
                then_wait(v.tensor_reduce(stat_b[:, :], src_t, AX.X, ALU.add))
                then_wait(v.tensor_scalar(stat_b[:, :], stat_b[:, :], 1.0 / H, None, ALU.mult))
                then_wait(v.tensor_tensor(dst_t, src_t, bc(stat_b[:, :]), ALU.subtract))
                then_wait(v.tensor_tensor(square, dst_t, dst_t, ALU.mult))
                then_wait(v.tensor_reduce(stat_b[:, :], square, AX.X, ALU.add))
                then_wait(v.tensor_scalar(stat[:, :], stat_b[:, :], 1.0 / H, LN_EPS, ALU.mult, ALU.add))
                root()
                then_wait(v.reciprocal(stat_b[:, :], std[:, :]))
                then_wait(v.tensor_tensor(dst_t, dst_t, bc(stat_b[:, :]), ALU.mult))

            v.wait_ge(row_stored_v, NB + 1)
            v.wait_ge(row_stored_a, NB + 1)
            then_wait(v.tensor_tensor(dis[:, :], deg2[:, 0, :], deg2[:, 1, :], ALU.add))
            then_wait(v.tensor_scalar(stat[:, :], dis[:, :], 2.0, 1.0, ALU.mult, ALU.max))
            root()
            then_wait(v.reciprocal(stat_b[:, :], std[:, :]))
            then_wait(v.scalar_tensor_tensor(out=dis[:, :], in0=dis[:, :], scalar=0.0, in1=stat_b[:, :], op0=ALU.is_gt, op1=ALU.mult))
            then_wait(v.tensor_scalar(stat_b[:, :], agg[:, :, H], 1e-8, None, ALU.max))
            then_wait(v.reciprocal(stat_b[:, :], stat_b[:, :]))
            then_wait(v.tensor_tensor(work, agg[:, :, :H], bc(stat_b[:, :]), ALU.mult))
            then_wait(v.tensor_tensor(work, work, xs[:, :, :], ALU.add))
            norm(prop, work)
            then_wait(v.tensor_tensor(prop, prop, all_blocks(gamma_all), ALU.mult))
            then_wait(v.tensor_tensor(prop, prop, all_blocks(beta_all), ALU.add))
            then_wait(v.tensor_tensor(work, prop, xs[:, :, :], ALU.add))
            norm(xs[:, :, :], work)

            t3 = orders[:, :, 3, :]
            terms = [xs[:, :, :], t1, t2, t3]
            for k in range(1, ORDERS):
                then_wait(v.tensor_tensor(work, terms[k - 1], bc(dis[:, :]), ALU.mult))
                then_wait(v.tensor_copy(parts[:, :, 0, :], work))
                then_wait(v.tensor_tensor(work, work, parts[:, :, 0, :], ALU.subtract))
                then_wait(v.tensor_copy(parts[:, :, 1, :], work))
                then_wait(v.tensor_tensor(work, work, parts[:, :, 1, :], ALU.subtract))
                then_wait(v.tensor_copy(parts[:, :, 2, :], work))
                v.sem_inc(split_ready, 1)
                with v.Fori(0, NB // 5) as i:
                    for j in range(5):
                        v.wait_ge(prop_ready, i * 5 + (k - 1) * NB + j + 1)
                        v.sem_inc(v_tick, 1)
                        v.tensor_reduce(prop[:, bass.ds(i * 5 + j, 1), :].rearrange("p b h -> p (b h)"),
                                        bk(j, 0, 3 * H).rearrange("p (s h) -> p h s", s=3), AX.X, ALU.add).then_inc(prop_read, 1)
                v.wait_ge(prop_read, k * NB + 5)
                then_wait(v.tensor_tensor(prop, prop, bc(dis[:, :]), ALU.mult))
                if k == 1:
                    then_wait(v.tensor_scalar(t1, prop, -2.0, None, ALU.mult))
                else:
                    then_wait(v.scalar_tensor_tensor(out=terms[k], in0=prop, scalar=-4.0, in1=terms[k - 2], op0=ALU.mult, op1=ALU.subtract))
            v.sem_inc(orders_ready, 1)
            then_wait(v.tensor_tensor(work, xs[:, :, :], all_blocks(bias_all), ALU.add))
            for c in range(-(-NB // 9)):
                lo, hi = 9 * c, min(9 * c + 9, NB)
                v.wait_ge(proj_ready, hi)
                then_wait(v.tensor_tensor(work[:, lo:hi, :], work[:, lo:hi, :], bk(c, 0, (hi - lo) * H).rearrange("p (b h) -> p b h", h=H), ALU.add))
            norm(xs[:, :, :], work)
            v.sem_inc(out_ready, 1)


def kernel(**inputs):
    import numpy as _np
    import concourse.bacc as _bacc
    from concourse import mybir as _mybir
    from concourse.bass_utils import run_bass_kernel_spmd as _run

    nc = _bacc.Bacc("TRN2", target_bir_lowering=False, num_devices=1)
    plan = [("x", 0), ("src", 0), ("dst", 0), ("edge_attr_40", 0), ("edge_weight", 0), ("node_type_119", 0), ("node_vec", 0),
            ("L0_gnn_W1", 1), ("L0_gnn_b1", 0), ("L0_gnn_W2", 1), ("L0_gnn_b2", 0), ("L0_gnn_emb", 1), ("L0_gnn_adaptW", 1),
            ("L0_gnn_gamma", 0), ("L0_gnn_beta", 0), ("L1_gnn_weight", 0), ("L1_gnn_bias", 0)]
    arrays, args = {}, []
    for name, turn in plan:
        a = _np.asarray(inputs[name])
        a = _np.ascontiguousarray(a.T if turn else a)
        arrays[f"in_{name}_dram"] = a
        args.append(nc.dram_tensor(f"in_{name}_dram", a.shape, _mybir.dt.from_np(a.dtype), kind="ExternalInput").ap())
    shape = _np.asarray(inputs["x"]).shape
    args.append(nc.dram_tensor("out_0_dram", shape, F32, kind="ExternalOutput").ap())
    gnn_program(nc, *args)
    r = _run(nc, [arrays], core_ids=[0])
    return r.results[0]["out_0_dram"]
```

```python
from contextlib import ExitStack

import concourse.bass as bass
from concourse import mybir

F32 = mybir.dt.float32
F16 = mybir.dt.float16
BF16 = mybir.dt.bfloat16
I32 = mybir.dt.int32
ALU = mybir.AluOpType
ACT = mybir.ActivationFunctionType
AX = mybir.AxisListType

P = 128
PI = 3.141592653589793
CUTOFF = 6.0
LN_EPS = 1e-5


def gnn_program(nc, x, src, dst, edge_attr, edge_weight, node_type, node_vec, w1t, b1, w2t, b2, embt,
                adaptwt, gamma, beta, cheb_w, cheb_bias, out):
    N, H = x.shape
    E, R = dst.shape[0], w1t.shape[0]
    EMB, NEL = embt.shape
    ORDERS = cheb_w.shape[0]
    NB = -(-N // P)
    LAST = N - (NB - 1) * P
    NPAD = NB * P
    GW = 512
    DG = -(-N // GW)
    BINS = NB * DG
    EP = 125
    NT = E // EP
    BODY = 33
    PC = 17
    GROUPS = 9
    TURNS = NT // BODY
    TILES = [range(4 * g, min(4 * g + 4, BODY)) for g in range(GROUPS)]
    COLS = [range(2 * g, min(2 * g + 2, PC)) for g in range(GROUPS)]
    LOADS = [(0, 6, 3), (6, 12, 6), (12, 17, 9)]
    RING = 11
    HT = 4 * (-(-NT // 4))
    HW = 32
    assert EP * NT == E and TURNS * BODY == NT and BODY % RING == 0
    U = 8
    HALF = U // 2
    SLOTS = 4
    TMAX = -(-(-(-E // P) + NB * max(DG + U - 1, 2 * U)) // U) * U + U
    QMAX = TMAX // U - 1
    TCOLS = U * (-(-(TMAX + HALF) // P // U))
    REC = H + 4
    CW, SLOC, DSTC, DLOC = H, H + 1, H + 2, H + 3
    SELF = 8192.0
    NTAB = 84
    HM, MULT = EMB, EMB + H
    NCH = NB * H
    CUT = 4 * GW

    rec_dram = nc.dram_tensor("rec_sorted", (TMAX * P, REC), F32).ap()
    node_dram = nc.dram_tensor("node_table", (NPAD, NTAB), F32).ap()
    type_dram = nc.dram_tensor("type_table", (NEL, 2 * EMB), F32).ap()
    hist_dram = nc.dram_tensor("hist_row", (1, BINS), F32).ap()
    unit_dram = nc.dram_tensor("unit_row", (1, P * TCOLS // U), I32).ap()

    with ExitStack() as ctx:
        def sb(name, shape, dt=F32):
            return ctx.enter_context(nc.sbuf_tensor(name, shape, dt))

        def sem(name):
            return ctx.enter_context(nc.semaphore(name))

        big = sb("big", [P, NB * NPAD // 2])
        counts = big[:, :].bitcast(F16).rearrange("p (b d) -> p b d", b=NB)
        top = [0]

        def part(n):
            top[0] += n
            assert top[0] <= NB * NPAD // 2
            return big[:, top[0] - n:top[0]]

        src_i = part(NT).bitcast(I32)[:EP]
        dst_i = part(NT).bitcast(I32)[:EP]
        tmp_i = part(NT).bitcast(I32)[:EP]
        tmp_j = part(NT).bitcast(I32)[:EP]
        dist = part(NT)[:EP]
        tmp_f = part(NT)[:EP]
        tmp_g = part(NT)[:EP]
        bin_f = part(NT + len(TILES[0]))[:EP]
        aux = part(NT * 4)[:EP].rearrange("p (t f) -> p t f", f=4)
        attr = part(PC * EP)[:2 * R]
        recs = part(BODY * REC)[:EP].rearrange("p (t f) -> p t f", f=REC)
        hid = [part(2 * EP)[:2 * H] for _ in range(2)]
        onehot_bin = [part(-(-BINS // 2)).bitcast(F16)[:EP, :BINS] for _ in range(RING)]
        pos_f = part(BODY)[:EP]
        pos_i = [part(4).bitcast(I32)[:EP] for _ in range(GROUPS)]
        pad_rec = part(8 * REC)
        iota_bin = part(-(-BINS // 2)).bitcast(F16)[:, :BINS]
        tri_lt = part(P // 2).bitcast(F16)
        tri_ge = part(P // 2).bitcast(F16)
        tri_all = part(P // 2).bitcast(F16)
        onehot_sb = part(HW * HT // 2).bitcast(F16)[:EP].rearrange("p (u b k) -> p u b k", b=HW, k=4)
        onehot_dg = part(DG * HT // 2).bitcast(F16)[:EP].rearrange("p (g t) -> p g t", g=DG)
        hist_mask = part(4)
        hist_own = part(4 * DG)
        hist_part = part(DG)
        fold = part(HW)
        bin_starts = part(BINS)
        sb_starts = part(NB)
        tile_ids = part(TCOLS)
        bin_count = part(TCOLS)
        sb_count = part(TCOLS)
        small_junk = part(BINS)
        unit_f = part(TCOLS // U)
        unit_i = part(TCOLS // U).bitcast(I32)
        ones_row = part(P)
        hist_sb = part(DG)
        row_f = part(BINS)
        row_i = part(BINS).bitcast(I32)
        row_t = part(BINS)
        row_start = part(BINS)
        rank_junk = [small_junk[:EP], row_t[:EP]]
        sb_tiles = part(NB)
        sb_end = part(NB)
        sb_first = part(NB)
        sb_i = part(NB).bitcast(I32)
        types = part(NB).bitcast(I32)
        iota_i = part(GW).bitcast(I32)
        tile_i = part(TCOLS).bitcast(I32)
        sb_h = part(HT // 2).bitcast(F16)[:EP]
        dg_h = part(-(-NT // 2)).bitcast(F16)[:EP, :NT]
        type_rows = part(NB * 2 * EMB).rearrange("p (b f) -> p b f", b=NB)
        nodes = part(NB * NTAB).rearrange("p (b f) -> p b f", b=NB)
        emb_rest = part(NB * EMB).rearrange("p (b e) -> p b e", b=NB)
        type_sb = part(2 * EMB)
        embt_sb = part(NEL)
        adaptwt_sb = part(EMB)

        ident = sb("ident", [P, P])
        ident_h = sb("ident_h", [P, P], F16)
        iota_d = sb("iota_d", [P, GW], F16)
        w1_pair = sb("w1_pair", [2 * R, 2 * H])
        w2_pair = sb("w2_pair", [2 * H, 2 * H])
        b1_pair = sb("b1_pair", [2 * H, 1])
        b2_all = sb("b2_all", [P, H])
        gamma_all = sb("gamma_all", [P, H])
        beta_all = sb("beta_all", [P, H])
        bias_all = sb("bias_all", [P, H])
        xs = sb("xs", [P, NB, H])
        mult = sb("mult", [P, NB])
        starts_i = sb("starts_i", [1, NB + 1], I32)
        lasts_i = sb("lasts_i", [1, NB], I32)
        unit_row = sb("unit_row_sb", [1, P * TCOLS // U], I32)
        half_pi = sb("half_pi", [P, 1])
        zeros_h = sb("zeros_h", [P, GW], F16)
        cheb_sb = sb("cheb_sb", [2 * H, ORDERS // 2, H])
        agg = sb("agg", [P, NB, H + 1])
        deg2 = sb("deg2", [P, 2, NB])
        dis = sb("dis", [P, NB])
        stat = sb("stat", [P, NB])
        stat_b = sb("stat_b", [P, NB])
        std = sb("std", [P, NB])

        MID = 2 * U * (REC + NTAB) + HALF * H + U * (EMB + 4 + P + P // 2 + GW // 2 + 2 * H + 2) + HALF * P // 2 + HALF * 3 * EMB + 3 * NB * EMB // 2
        mid = sb("mid", [P, max(MID, 5 * NCH + 3 * NCH // 2)])
        used = [0]

        def mid_part(n):
            used[0] += n
            return mid[:, used[0] - n:used[0]]

        rin = mid_part(2 * U * REC).rearrange("p (r j f) -> p r j f", r=2, j=U)
        ngath = mid_part(2 * U * NTAB).rearrange("p (r j f) -> p r j f", r=2, j=U)
        gated = mid_part(HALF * H).rearrange("p (j f) -> p j f", j=HALF)
        query = mid_part(U * EMB).rearrange("p (j f) -> p j f", j=U)
        meta = mid_part(U * 4).rearrange("p (j f) -> p j f", j=U)
        hot_s = mid_part(U * P).rearrange("p (j s) -> p j s", j=U)
        hot_sh = mid_part(U * P // 2).bitcast(F16).rearrange("p (j s) -> p j s", j=U)
        hot_st = mid_part(HALF * P // 2).bitcast(F16).rearrange("p (j s) -> p j s", j=HALF)
        hot_d = mid_part(U * GW // 2).bitcast(F16).rearrange("p (j s) -> p j s", j=U)
        msg_pre = mid_part(U * H).rearrange("p (j s) -> p j s", j=U)
        msg = mid_part(U * (H + 1)).rearrange("p (j s) -> p j s", j=U)
        adapt = mid_part(U)
        adapt_junk = mid_part(HALF * 3 * EMB).rearrange("p (k s e) -> p k s e", k=HALF, s=3)
        emb_parts = mid_part(3 * NB * EMB // 2).bitcast(BF16).rearrange("p (b f) -> p b f", b=NB)
        used[0] = 0

        def node_part(n=NCH):
            return mid_part(n).rearrange("p (b h) -> p b h", b=NB)

        t1, t2, prop, work, square = [node_part() for _ in range(5)]
        parts = mid_part(3 * NCH // 2).bitcast(BF16).rearrange("p (b s h) -> p b s h", b=NB, s=3)
        orders = big[:, :ORDERS * NCH].rearrange("p (b k h) -> p b k h", b=NB, k=ORDERS)
        turned = [big[:2 * H, ORDERS * NCH + j * 2 * P:ORDERS * NCH + (j + 1) * 2 * P].rearrange("p (k n) -> p k n", k=2) for j in range(2)]

        psum = ctx.enter_context(nc.psum_tensor("psum", [P, 8 * GW], F32))

        def bk(b, lo, hi, rows=P):
            return psum[:rows, b * GW + lo:b * GW + hi]

        AGG0 = (DG - 1) * GW + P

        small_loaded = sem("small_loaded")
        edges_loaded = sem("edges_loaded")
        v_step = sem("v_step")
        a_step = sem("a_step")
        g_step = sem("g_step")
        iotas_ready = sem("iotas_ready")
        hots_ready = sem("hots_ready")
        hist_ready = sem("hist_ready")
        own_ready = sem("own_ready")
        hist_folded = sem("hist_folded")
        hist_copied = sem("hist_copied")
        hist_moved = sem("hist_moved")
        starts_ready = sem("starts_ready")
        bcast_ready = sem("bcast_ready")
        units_ready = sem("units_ready")
        units_moved = sem("units_moved")
        type_ready = sem("type_ready")
        type_copied = sem("type_copied")
        type_moved = sem("type_moved")
        types_gathered = sem("types_gathered")
        nodes_ready = sem("nodes_ready")
        nodes_moved = sem("nodes_moved")
        angle_ready = sem("angle_ready")
        sine_ready = sem("sine_ready")
        pad_ready = sem("pad_ready")
        attr_loaded = [sem(f"attr_loaded{s}") for s in range(len(LOADS))]
        hid_ready = sem("hid_ready")
        silu_done = sem("silu_done")
        gate_ready = sem("gate_ready")
        gate_copied = sem("gate_copied")
        bin_hot = sem("bin_hot")
        rank_ready = sem("rank_ready")
        rank_read = sem("rank_read")
        rank_added = sem("rank_added")
        pool_tick = sem("pool_tick")
        scattered = [sem(f"scattered{g}") for g in range(GROUPS)]
        rec_loaded = [sem(f"rec_loaded{s}") for s in range(SLOTS)]
        gathered = [sem(f"gathered{s}") for s in range(SLOTS)]
        recs_in = sem("recs_in")
        rows_in = sem("rows_in")
        meta_ready = sem("meta_ready")
        query_ready = sem("query_ready")
        gated_ready = sem("gated_ready")
        hot_ready = sem("hot_ready")
        counted = sem("counted")
        hot_turned = sem("hot_turned")
        hot_copied = sem("hot_copied")
        emb_ready = sem("emb_ready")
        adapt_done = sem("adapt_done")
        pre_ready = sem("pre_ready")
        msg_ready = sem("msg_ready")
        summed = sem("summed")
        row_stored_v = sem("row_stored_v")
        row_stored_a = sem("row_stored_a")
        agg_stored = sem("agg_stored")
        var_ready = sem("var_ready")
        std_ready = sem("std_ready")
        split_ready = sem("split_ready")
        prop_ready = sem("prop_ready")
        prop_read = sem("prop_read")
        turn_ready = sem("turn_ready")
        turn_copied = sem("turn_copied")
        proj_ready = sem("proj_ready")
        orders_copied = sem("orders_copied")
        act_tick = sem("act_tick")
        pe_tick = sem("pe_tick")
        sp_tick = sem("sp_tick")
        v_tick = sem("v_tick")
        orders_ready = sem("orders_ready")
        out_ready = sem("out_ready")
        stored = sem("stored")

        def row_of(v):
            return v.rearrange("(a n) -> a n", a=1)

        xb = x[:(NB - 1) * P].rearrange("(b p) h -> p b h", p=P)
        outb = out[:(NB - 1) * P].rearrange("(b p) h -> p b h", p=P)
        SMALL = 12 + ORDERS // 2 + 6

        block = ctx.enter_context(nc.Block())

        @block.sync
        def _(sp):
            sp.dma_start(src_i, src.rearrange("(p t) -> p t", p=EP)).then_inc(edges_loaded, 16)
            sp.dma_start(dst_i, dst.rearrange("(p t) -> p t", p=EP)).then_inc(edges_loaded, 16)
            sp.dma_start(dist, edge_weight.rearrange("(p t) -> p t", p=EP)).then_inc(edges_loaded, 16)
            sp.dma_start(embt_sb[:EMB], embt).then_inc(small_loaded, 16)
            sp.dma_start(adaptwt_sb[:EMB], adaptwt).then_inc(small_loaded, 16)
            sp.dma_start(b2_all[:, :], row_of(b2).to_broadcast([P, H])).then_inc(small_loaded, 16)
            sp.dma_start(gamma_all[:, :], row_of(gamma).to_broadcast([P, H])).then_inc(small_loaded, 16)
            sp.dma_start(beta_all[:, :], row_of(beta).to_broadcast([P, H])).then_inc(small_loaded, 16)
            sp.dma_start(bias_all[:, :], row_of(cheb_bias).to_broadcast([P, H])).then_inc(small_loaded, 16)
            for k in range(ORDERS // 2):
                sp.dma_start(cheb_sb[:, k, :], cheb_w[2 * k:2 * k + 2].rearrange("k i o -> (k i) o")).then_inc(small_loaded, 16)
            sp.wait_ge(pad_ready, 1)
            for k in range(2):
                sp.dma_start(w1_pair[k * R:(k + 1) * R, k * H:(k + 1) * H], w1t).then_inc(small_loaded, 16)
                sp.dma_start(w2_pair[k * H:(k + 1) * H, k * H:(k + 1) * H], w2t).then_inc(small_loaded, 16)
                sp.dma_start(b1_pair[k * H:(k + 1) * H, :], b1.rearrange("(h a) -> h a", a=1)).then_inc(small_loaded, 16)
            sp.dma_start(xs[:, :NB - 1, :], xb).then_inc(small_loaded, 16)
            sp.dma_start(xs[:LAST, NB - 1, :], x[(NB - 1) * P:]).then_inc(small_loaded, 16)
            sp.dma_start(mult[:, :NB - 1], node_vec[:(NB - 1) * P].rearrange("(b p) -> p b", p=P),
                         allow_slow_non_contiguous=True).then_inc(small_loaded, 16)
            sp.dma_start(mult[:LAST, NB - 1:NB], node_vec[(NB - 1) * P:].rearrange("(p a) -> p a", a=1)).then_inc(small_loaded, 16)
            sp.dma_start(types[:, :NB - 1], node_type[:(NB - 1) * P].rearrange("(b p) -> p b", p=P),
                         allow_slow_non_contiguous=True).then_inc(small_loaded, 16)
            sp.dma_start(types[:LAST, NB - 1:NB], node_type[(NB - 1) * P:].rearrange("(p a) -> p a", a=1)).then_inc(small_loaded, 16)
            for s, (lo, hi, _) in enumerate(LOADS):
                sp.dma_start(attr[:, lo * EP:hi * EP], edge_attr[0, :, lo * EP:hi * EP]).then_inc(attr_loaded[s], 16)
            sp.wait_ge(type_copied, 1)
            sp.dma_start(type_dram, type_sb[:NEL]).then_inc(type_moved, 16)
            sp.wait_ge(hist_copied, 1)
            sp.dma_start(hist_dram.rearrange("a (b g) -> (a b) g", b=NB), hist_sb[:NB]).then_inc(hist_moved, 16)
            sp.wait_ge(hist_moved, 16)
            sp.dma_start(row_f[:1], hist_dram).then_inc(hist_moved, 16)
            sp.wait_ge(nodes_ready, 1)
            sp.dma_start(node_dram.rearrange("(b p) f -> p b f", p=P), nodes).then_inc(nodes_moved, 16)
            sp.wait_ge(units_ready, 1)
            sp.dma_start(unit_dram.rearrange("a (p c) -> (a p) c", p=P), unit_i).then_inc(units_moved, 16)
            sp.wait_ge(units_moved, 16)
            sp.dma_start(unit_row[:, :], unit_dram).then_inc(units_moved, 16)
            with sp.Fori(1, TURNS) as i:
                for s, (lo, hi, used_by) in enumerate(LOADS):
                    sp.wait_ge(hid_ready, (i - 1) * GROUPS + used_by)
                    sp.dma_start(attr[:, lo * EP:hi * EP], edge_attr[bass.ds(i, 1), :, lo * EP:hi * EP].rearrange("i r e -> (i r) e")).then_inc(attr_loaded[s], 16)
            for g in range(GROUPS):
                sp.wait_ge(scattered[g], 16 + 16 * len(TILES[g]) * TURNS)
            turns = sp.value_load(starts_i[0:1, NB:NB + 1], min_val=1, max_val=QMAX)
            halves = rec_dram.rearrange("(k j p) f -> p k j f", p=P, j=HALF)

            def load(k, slot):
                sp.dma_start(rin[:, slot // 2, slot % 2 * HALF:(slot % 2 + 1) * HALF, :],
                             halves[:, bass.ds(k, 1), :, :].rearrange("p k j f -> p (k j) f")).then_inc(rec_loaded[slot], 16)

            def turn_in(q, use, r):
                for h in range(2):
                    sp.wait_ge(msg_ready, q * U + (h + 3) * HALF)
                    sp.sem_inc(sp_tick, 1)
                    load(q * 2 + h + 2, 2 * (1 - r) + h)
                    sp.wait_ge(rec_loaded[2 * (1 - r) + h], use * 16 + 16 * (r + 1))
                    sp.sem_inc(recs_in, 1)
                    sp.wait_ge(gathered[2 * r + h], use * (16 * HALF) + 16 * HALF)
                    sp.sem_inc(rows_in, 1)

            for h in range(2):
                load(h, h)
                sp.wait_ge(rec_loaded[h], 16)
                sp.sem_inc(recs_in, 1)
            with sp.Fori(0, turns // 2) as i:
                for r in range(2):
                    turn_in(i * 2 + r, i, r)
            with sp.Fori(turns // 2, (turns + 1) // 2) as i:
                turn_in(i * 2, i, 0)
            sp.wait_ge(out_ready, 1)
            sp.dma_start(outb, xs[:, :NB - 1, :]).then_inc(stored, 16)
            sp.dma_start(out[(NB - 1) * P:], xs[:LAST, NB - 1, :]).then_inc(stored, 16)
            sp.wait_ge(stored, 32)

        @block.gpsimd
        def _(gp):
            n = 0

            def then_wait(inst):
                nonlocal n
                n += 1
                inst.then_inc(g_step, 1)
                gp.wait_ge(g_step, n)

            then_wait(gp.memset(xs[:, NB - 1, :], 0.0))
            then_wait(gp.memset(mult[:, NB - 1:NB], 0.0))
            then_wait(gp.memset(types[:, NB - 1:NB], 0))
            then_wait(gp.memset(pad_rec, 0.0))
            padv = pad_rec.rearrange("p (k f) -> p k f", f=REC)
            then_wait(gp.memset(padv[:, :, SLOC], -1.0))
            then_wait(gp.memset(padv[:, :, DLOC], SELF))
            then_wait(gp.memset(w1_pair[:, :], 0.0))
            then_wait(gp.memset(w2_pair[:, :], 0.0))
            gp.sem_inc(pad_ready, 1)
            then_wait(gp.iota(iota_i, [[1, GW]], base=0, channel_multiplier=0))
            then_wait(gp.tensor_copy(iota_d[:, :], iota_i))
            then_wait(gp.tensor_copy(iota_bin, iota_i[:, :BINS]))
            then_wait(gp.iota(tile_i, [[1, TCOLS]], base=-HALF, channel_multiplier=TCOLS))
            then_wait(gp.tensor_copy(tile_ids, tile_i))
            then_wait(gp.memset(zeros_h[:, :], 0.0))
            then_wait(gp.memset(ones_row, 1.0))
            then_wait(gp.memset(hid[0], 0.0))
            then_wait(gp.memset(nodes[:, :, MULT + 1:], 0.0))
            then_wait(gp.memset(half_pi[:, :], PI / 2))
            then_wait(gp.memset(tri_all, 1.0))
            then_wait(gp.memset(tri_ge, 1.0))
            then_wait(gp.affine_select(tri_lt, tri_ge, [[1, P]], ALU.is_gt, 0.0, base=0, channel_multiplier=-1))
            then_wait(gp.affine_select(tri_ge, tri_ge, [[-1, P]], ALU.is_ge, 0.0, base=0, channel_multiplier=1))
            then_wait(gp.memset(ident[:, :], 1.0))
            then_wait(gp.affine_select(ident[:, :], ident[:, :], [[1, P]], ALU.is_equal, 0.0, base=0, channel_multiplier=-1))
            then_wait(gp.tensor_copy(ident_h[:, :], ident[:, :]))
            gp.sem_inc(iotas_ready, 1)
            gp.wait_ge(small_loaded, SMALL * 16)
            gp.wait_ge(type_moved, 16)
            for b in range(NB):
                gp.indirect_dma_start(type_rows[:, b, :], None, type_dram, bass.IndirectOffsetOnAxis(ap=types[:, b:b + 1], axis=0)).then_inc(types_gathered, 16)
            for g in range(GROUPS):
                lo, hi = TMAX // 8 * g // GROUPS * 8, TMAX // 8 * (g + 1) // GROUPS * 8
                gp.dma_start(rec_dram[lo * P:hi * P].rearrange("(c p k) f -> p c (k f)", p=P, k=8),
                             pad_rec.unsqueeze(1).to_broadcast([P, (hi - lo) // 8, 8 * REC])).then_inc(scattered[g], 16)
            for g in range(GROUPS):
                gp.wait_ge(scattered[g], 16)
            with gp.Fori(0, TURNS) as i:
                for g in range(GROUPS):
                    gp.wait_ge(gate_copied, i * GROUPS + g + 4)
                    gp.sem_inc(pool_tick, 1)
                    for k, t in enumerate(TILES[g]):
                        gp.indirect_dma_start(rec_dram, bass.IndirectOffsetOnAxis(ap=pos_i[g][:, k:k + 1], axis=0),
                                              recs[:, t, :], None).then_inc(scattered[g], 16)
            gp.wait_ge(nodes_moved, 16)
            gp.wait_ge(starts_ready, 1)
            last = gp.value_load(starts_i[0:1, NB:NB + 1], min_val=1, max_val=QMAX)
            def turn_gathers(q, r):
                for h in range(2):
                    gp.wait_ge(recs_in, q * 2 + h + 1)
                    gp.sem_inc(pool_tick, 1)
                    for j in range(h * HALF, (h + 1) * HALF):
                        gp.indirect_dma_start(ngath[:, r, j, :], None, node_dram, bass.IndirectOffsetOnAxis(ap=rin[:, r, j, DSTC:DSTC + 1].bitcast(I32), axis=0)).then_inc(gathered[2 * r + h], 16)

            with gp.Fori(0, last // 2) as i:
                for r in range(2):
                    turn_gathers(i * 2 + r, r)
            with gp.Fori(last // 2, (last + 1) // 2) as i:
                turn_gathers(i * 2, 0)

        @block.scalar
        def _(act):
            n = 0

            def then_wait(inst):
                nonlocal n
                n += 1
                inst.then_inc(a_step, 1)
                act.wait_ge(a_step, n)

            act.sem_inc(silu_done, 1)
            act.sem_inc(msg_ready, 2 * U)
            act.wait_ge(iotas_ready, 1)
            act.wait_ge(angle_ready, 1)
            act.activation(tmp_g, tmp_f, ACT.Sin, bias=half_pi[:EP, :], scale=-PI / CUTOFF).then_inc(sine_ready, 1)
            act.wait_ge(type_ready, 1)
            then_wait(act.copy(type_sb[:NEL], bk(0, 0, 2 * EMB, NEL)))
            act.sem_inc(type_copied, 1)
            act.wait_ge(small_loaded, SMALL * 16)
            with act.Fori(0, TURNS) as i:
                for g in range(GROUPS):
                    n1 = len(COLS[g]) * EP
                    act.wait_ge(hid_ready, i * GROUPS + g + 1)
                    act.wait_ge(gate_ready, i * GROUPS + max(g - 1, 0) + 1)
                    act.activation(hid[g % 2][:, :n1], bk(2 + g % 2, 0, n1, 2 * H), ACT.Silu, bias=b1_pair[:, :]).then_inc(silu_done, 1)
            act.sem_inc(row_stored_a, 1)
            act.wait_ge(starts_ready, 1)
            def next_metas(q, h):
                act.wait_ge(recs_in, q * 2 + h + 3)
                act.sem_inc(act_tick, 1)
                act.wait_ge(counted, q * 2 + h + 3)
                act.sem_inc(act_tick, 1)
                act.copy(meta[:, h * HALF:(h + 1) * HALF, :], rin[:, bass.ds((q + 1) % 2, 1), h * HALF:(h + 1) * HALF, H:].rearrange("p r j f -> p (r j) f")).then_inc(meta_ready, 1)

            def turned_out(q, h):
                act.wait_ge(hot_turned, q * 2 + h + 1)
                act.sem_inc(act_tick, 1)
                act.wait_ge(emb_ready, q * 2 + h + 1)
                act.copy(hot_st, bk(7, 0, HALF * P // 2).bitcast(F16).rearrange("p (j s) -> p j s", j=HALF)).then_inc(hot_copied, 1)

            def widen(q, h):
                act.wait_ge(hot_ready, q * U + (h + 1) * HALF)
                act.sem_inc(act_tick, 1)
                act.wait_ge(summed, q * U + (h + 1) * HALF)
                act.copy(hot_s[:, h * HALF:(h + 1) * HALF, :], hot_sh[:, h * HALF:(h + 1) * HALF, :])

            def queries(q, h):
                act.wait_ge(rows_in, q * 2 + h + 1)
                act.sem_inc(act_tick, 1)
                act.wait_ge(msg_ready, q * U + (h + 1) * HALF + U)
                act.sem_inc(act_tick, 1)
                act.copy(query[:, h * HALF:(h + 1) * HALF, :], ngath[:, bass.ds(q % 2, 1), h * HALF:(h + 1) * HALF, :EMB].rearrange("p r j f -> p (r j) f")).then_inc(query_ready, 1)

            def weigh(q, h):
                js = range(h * HALF, (h + 1) * HALF)
                act.wait_ge(pre_ready, q * 2 + h + 1)
                act.sem_inc(act_tick, 1)
                r = bass.ds(q % 2, 1)
                act.copy(msg[:, js[0]:js[-1] + 1, H:], ngath[:, r, js[0]:js[-1] + 1, MULT:MULT + 1].rearrange("p r j f -> p (r j) f"))
                for j in js:
                    act.activation(msg[:, j, :H], msg_pre[:, j, :], ACT.Copy, scale=rin[:, r, j, CW:CW + 1].rearrange("p r f -> p (r f)")).then_inc(msg_ready, 1)

            for h in range(2):
                act.wait_ge(recs_in, h + 1)
                act.copy(meta[:, h * HALF:(h + 1) * HALF, :], rin[:, 0, h * HALF:(h + 1) * HALF, H:]).then_inc(meta_ready, 1)
            act.wait_ge(hot_turned, 1)
            act.wait_ge(emb_ready, 1)
            act.copy(hot_st, bk(7, 0, HALF * P // 2).bitcast(F16).rearrange("p (j s) -> p j s", j=HALF)).then_inc(hot_copied, 1)
            act.wait_ge(hot_ready, HALF)
            act.copy(hot_s[:, :HALF, :], hot_sh[:, :HALF, :])
            with act.Fori(0, NB) as b:
                q0 = act.value_load(starts_i[0:1, bass.ds(b, 1)], min_val=0, max_val=QMAX - 2)
                ql = act.value_load(lasts_i[0:1, bass.ds(b, 1)], min_val=1, max_val=QMAX - 1)
                with act.Fori(q0, ql + 1) as q:
                    queries(q, 0)
                    turned_out(q, 1)
                    next_metas(q, 0)
                    weigh(q, 0)
                    widen(q, 1)
                    queries(q, 1)
                    turned_out(q + 1, 0)
                    next_metas(q, 1)
                    weigh(q, 1)
                    widen(q + 1, 0)
                act.wait_ge(summed, ql * U + 2 * U)
                act.sem_inc(act_tick, 1)
                act.activation(counts[:, bass.ds(b, 1), :CUT].rearrange("p b d -> p (b d)"), psum[:, :CUT], ACT.Copy, scale=0.5,
                               accum_out=deg2[:, 0, bass.ds(b, 1)]).then_inc(row_stored_a, 1)
            for k in range(3):
                act.wait_ge(var_ready, k + 1)
                act.activation(std[:, :], stat[:, :], ACT.Sqrt).then_inc(std_ready, 1)
            act.wait_ge(orders_ready, 1)
            for k, t in enumerate((xs[:, :, :], t1, t2)):
                act.copy(orders[:, :, k, :], t).then_inc(orders_copied, 1)
            for b in range(NB):
                act.wait_ge(turn_ready, b + 1)
                if b >= 2:
                    act.wait_ge(proj_ready, b - 1)
                act.copy(turned[b % 2], bk(5 + b % 2, 0, 2 * P, 2 * H).rearrange("p (k n) -> p k n", k=2)).then_inc(turn_copied, 1)
            act.wait_ge(var_ready, 4)
            act.activation(std[:, :], stat[:, :], ACT.Sqrt).then_inc(std_ready, 1)

        @block.tensor
        def _(pe):
            pe.sem_inc(rank_added, RING)
            pe.sem_inc(emb_ready, 1)
            pe.sem_inc(summed, U)
            pe.sem_inc(counted, 2)
            pe.wait_ge(iotas_ready, 1)
            pe.wait_ge(small_loaded, SMALL * 16)
            pe.matmul(bk(0, 0, EMB, NEL), embt_sb[:EMB], adaptwt_sb[:EMB], start=True, stop=True)
            pe.transpose(bk(0, EMB, 2 * EMB, NEL), embt_sb[:EMB], ident[:EMB, :EMB]).then_inc(type_ready, 1)
            pe.wait_ge(hots_ready, 1)
            pe.matmul(bk(1, 0, 4 * DG), zeros_h[:, :P], zeros_h[:, :4 * DG], start=True, stop=False, skip_group_check=True)
            with pe.Fori(0, HT // 36) as i:
                for j in range(9):
                    pe.matmul(bk(1, 0, 4 * DG), onehot_sb[:, bass.ds(i * 9 + j, 1), :, :].rearrange("p u b k -> p (u b k)"),
                              onehot_dg[:, :, bass.ds(i * 36 + j * 4, 4)].rearrange("p g t -> p t g"), start=False, stop=False, skip_group_check=True)
            pe.matmul(bk(1, 0, 4 * DG), zeros_h[:, :P], zeros_h[:, :4 * DG], start=False, stop=True, skip_group_check=True).then_inc(hist_ready, 1)
            pe.wait_ge(own_ready, 1)
            pe.matmul(bk(3, 0, DG, HW), fold, hist_part, start=True, stop=True).then_inc(hist_folded, 1)
            pe.wait_ge(starts_ready, 1)
            pe.matmul(bk(0, 0, BINS), ones_row[:1], row_start[:1], start=True, stop=True)
            pe.matmul(bk(0, BINS, BINS + NB), ones_row[:1], sb_first[:1], start=True, stop=True).then_inc(bcast_ready, 1)
            for bank in (6, 7):
                pe.matmul(bk(bank, 0, BINS, EP), ones_row[:1, :EP], row_f[:1], start=True, stop=False, skip_group_check=True)

            def add_bins(bank, edges, t):
                return pe.matmul(bk(bank, 0, BINS, EP), edges[:EP, :EP], onehot_bin[t % RING], start=False, stop=False, skip_group_check=True)

            pe.wait_ge(bin_hot, 1)
            add_bins(6, tri_lt, 0).then_inc(rank_ready, 1)
            add_bins(7, tri_all, 0)
            pe.wait_ge(bin_hot, 2)
            add_bins(7, tri_lt, 1).then_inc(rank_ready, 1)

            with pe.Fori(0, TURNS) as i:
                def even(t):
                    pe.wait_ge(rank_read, i * BODY + t + 1)
                    add_bins(6, tri_ge, t).then_inc(rank_added, 1)
                    if t + 1 < BODY:
                        add_bins(6, tri_all, t + 1)
                    after = t + 2 if t + 1 < BODY else BODY
                    pe.wait_ge(bin_hot, i * BODY + after + 1)
                    add_bins(6, tri_lt, after % BODY).then_inc(rank_ready, 1)

                def odd(t):
                    if t < BODY:
                        pe.wait_ge(rank_read, i * BODY + t + 1)
                        add_bins(7, tri_ge, t).then_inc(rank_added, 1)
                    add_bins(7, tri_all, min(t + 1, BODY) % BODY)
                    if t + 1 != BODY - 1:
                        after = min(t + 2, BODY + 1)
                        pe.wait_ge(bin_hot, i * BODY + after + 1)
                        add_bins(7, tri_lt, after % BODY).then_inc(rank_ready, 1)

                def gate_of(g, c):
                    return pe.matmul(bk(4 + g % 2, c * 2 * H, (c + 1) * 2 * H, EP), hid[g % 2][:, c * EP:(c + 1) * EP], w2_pair[:, :], start=True, stop=True)

                for g in range(GROUPS):
                    ts = TILES[g]
                    last = (g - 1) % GROUPS
                    even(ts[0])
                    odd(ts[0] + 1)
                    pe.wait_ge(silu_done, i * GROUPS + g + 1)
                    pe.sem_inc(pe_tick, 1)
                    pe.wait_ge(gate_copied, i * GROUPS + (max(g - 2, 0) if g else -2) + 3)
                    for c in range(len(COLS[last])):
                        mm = gate_of(last, c)
                    mm.then_inc(gate_ready, 1)
                    if len(ts) > 1:
                        even(ts[2])
                        odd(ts[3])
                    for s, (lo, _, _) in enumerate(LOADS):
                        if COLS[g][0] == lo:
                            pe.wait_ge(attr_loaded[s], i * 16 + 16)
                            pe.sem_inc(pe_tick, 1)
                    pe.wait_ge(silu_done, i * GROUPS + max(g - 1, 0) + 1)
                    n1 = len(COLS[g]) * EP
                    pe.matmul(bk(2 + g % 2, 0, n1, 2 * H), w1_pair[:, :], attr[:, COLS[g][0] * EP:COLS[g][0] * EP + n1], start=True, stop=True).then_inc(hid_ready, 1)
            pe.wait_ge(silu_done, TURNS * GROUPS + 1)
            pe.wait_ge(gate_copied, (TURNS - 1) * GROUPS + GROUPS - 2 + 3)
            pe.matmul(bk(4 + (GROUPS - 1) % 2, 0, 2 * H, EP), hid[(GROUPS - 1) % 2][:, :EP], w2_pair[:, :], start=True, stop=True).then_inc(gate_ready, 1)

            pe.wait_ge(units_moved, 32)
            def turn(q, h):
                pe.wait_ge(hot_ready, q * U + (h + 1) * HALF)
                pe.sem_inc(pe_tick, 1)
                pe.wait_ge(adapt_done, q * U + h * HALF + HALF)
                for k in range(HALF):
                    mm = pe.transpose(bk(7, k * P // 2, (k + 1) * P // 2).bitcast(F16), hot_sh[:, h * HALF + k, :], ident_h[:, :])
                mm.then_inc(hot_turned, 1)

            pe.wait_ge(hot_ready, HALF)
            pe.wait_ge(adapt_done, HALF)
            for k in range(HALF):
                mm = pe.transpose(bk(7, k * P // 2, (k + 1) * P // 2).bitcast(F16), hot_sh[:, k, :], ident_h[:, :])
            mm.then_inc(hot_turned, 1)
            with pe.Fori(0, NB) as b:
                q0 = pe.value_load(starts_i[0:1, bass.ds(b, 1)], min_val=0, max_val=QMAX - 2)
                ql = pe.value_load(lasts_i[0:1, bass.ds(b, 1)], min_val=1, max_val=QMAX - 1)
                def groups(q):
                    return pe.value_load(unit_row[0:1, bass.ds(q, 1)], min_val=0, max_val=8 ** U - 1)

                def count(q, h, code):
                    for k in range(HALF):
                        j = h * HALF + k
                        pe.wait_ge(hot_ready, q * U + j + 1)
                        column = pe.snap((code // 8 ** (k + (1 - h) * HALF)) % 8, min_val=0, max_val=DG - 1)
                        mm = pe.matmul(psum[:, bass.ds(column * GW, GW)], hot_sh[:, j, :], hot_d[:, j, :], start=False, stop=False, skip_group_check=True)
                    mm.then_inc(counted, 1)

                def embed(q, h):
                    pe.wait_ge(hot_copied, q * 2 + h + 1)
                    for k in range(HALF):
                        mm = pe.matmul(bk(7, k * 3 * EMB, (k + 1) * 3 * EMB), hot_st[:, k, :],
                                       emb_parts[:, bass.ds(b, 1), :].rearrange("p b e -> p (b e)"), start=True, stop=True)
                    mm.then_inc(emb_ready, 1)

                def add_messages(q, h):
                    for j in range(h * HALF, (h + 1) * HALF):
                        pe.wait_ge(msg_ready, q * U + j + 1 + 2 * U)
                        pe.matmul(psum[:, AGG0:AGG0 + H + 1], hot_s[:, j, :], msg[:, j, :], start=False, stop=False, skip_group_check=True).then_inc(summed, 1)

                embed(q0, 0)
                pe.wait_ge(row_stored_v, b + 1)
                for g in range(CUT // GW, DG):
                    pe.matmul(bk(g, 0, GW), zeros_h[:, :P], zeros_h[:, :], start=True, stop=False, skip_group_check=True)
                pe.wait_ge(row_stored_a, b + 1)
                for g in range(CUT // GW):
                    pe.matmul(bk(g, 0, GW), zeros_h[:, :P], zeros_h[:, :], start=True, stop=False, skip_group_check=True)
                count(q0, 0, groups(q0))
                with pe.Fori(q0, ql) as q:
                    code = groups(q + 1)
                    turn(q, 1)
                    count(q, 1, code)
                    embed(q, 1)
                    add_messages(q, 0)
                    turn(q + 1, 0)
                    count(q + 1, 0, code)
                    embed(q + 1, 0)
                    add_messages(q, 1)
                turn(ql, 1)
                count(ql, 1, groups(ql + 1))
                embed(ql, 1)
                add_messages(ql, 0)
                turn(ql + 1, 0)
                add_messages(ql, 1)

            pe.wait_ge(row_stored_v, NB + 1)
            pe.wait_ge(row_stored_a, NB + 1)
            for k in range(1, ORDERS):
                pe.wait_ge(split_ready, k)
                with pe.Fori(0, NB // 5) as i:
                    for j in range(5):
                        pe.wait_ge(prop_read, i * 5 + (k - 1) * NB + j + 1)
                        for s in range(NB):
                            mm = pe.matmul(bk(j, 0, 3 * H), counts[:, s, bass.ds((i * 5 + j) * P, P)], parts[:, s, :, :].rearrange("p s h -> p (s h)"), start=(s == 0), stop=(s == NB - 1))
                        mm.then_inc(prop_ready, 1)
            pe.wait_ge(orders_ready, 1)
            pe.wait_ge(orders_copied, 3)
            for b in range(NB):
                if b >= 2:
                    pe.wait_ge(turn_copied, b - 1)
                for k in range(2):
                    mm = pe.transpose(bk(5 + b % 2, k * P, (k + 1) * P, 2 * H), orders[:, b, 2 * k:2 * k + 2, :].rearrange("p k h -> p (k h)"), ident[:, :])
                mm.then_inc(turn_ready, 1)
                pe.wait_ge(turn_copied, b + 1)
                o = b % 9 * H
                pe.matmul(bk(b // 9, o, o + H), turned[b % 2][:, 0, :], cheb_sb[:, 0, :], start=True, stop=False)
                pe.matmul(bk(b // 9, o, o + H), turned[b % 2][:, 1, :], cheb_sb[:, 1, :], start=False, stop=True).then_inc(proj_ready, 1)

        @block.vector
        def _(v):
            n = 0

            def then_wait(inst):
                nonlocal n
                n += 1
                inst.then_inc(v_step, 1)
                v.wait_ge(v_step, n)

            v.sem_inc(gate_copied, 2)
            v.sem_inc(adapt_done, HALF)
            v.sem_inc(prop_read, 5)
            v.wait_ge(edges_loaded, 3 * 16)
            v.memset(onehot_sb[:, :, NB:, :], 0.0)
            then_wait(v.memset(onehot_dg[:, :, NT:], 0.0))
            then_wait(v.tensor_scalar(tmp_i, src_i, 7, None, ALU.logical_shift_right))
            then_wait(v.tensor_scalar(tmp_j, dst_i, 9, None, ALU.logical_shift_right))
            v.memset(sb_h[:, NT:], -1.0)
            then_wait(v.tensor_copy(sb_h[:, :NT], tmp_i))
            then_wait(v.tensor_copy(dg_h, tmp_j))
            for b in range(NB):
                v.tensor_scalar(onehot_sb[:, :, b, :], sb_h.rearrange("p (u k) -> p u k", k=4), float(b), None, ALU.is_equal)
            for g in range(DG - 1):
                v.tensor_scalar(onehot_dg[:, g, :NT], dg_h, float(g), None, ALU.is_equal)
            then_wait(v.tensor_scalar(onehot_dg[:, DG - 1, :NT], dg_h, float(DG - 1), None, ALU.is_equal))
            v.sem_inc(hots_ready, 1)
            then_wait(v.memset(bin_f[:, NT:], -1.0))
            then_wait(v.scalar_tensor_tensor(out=bin_f[:, :NT], in0=tmp_i, scalar=float(DG), in1=tmp_j, op0=ALU.mult, op1=ALU.add))
            then_wait(v.scalar_tensor_tensor(out=tmp_g, in0=dist, scalar=-1.0, in1=dist, op0=ALU.mult, op1=ALU.max))
            then_wait(v.tensor_scalar(tmp_i, tmp_g, 1.0 / (2 * CUTOFF), None, ALU.mult))
            then_wait(v.scalar_tensor_tensor(out=tmp_f, in0=tmp_i, scalar=-2 * CUTOFF, in1=tmp_g, op0=ALU.mult, op1=ALU.add))
            then_wait(v.scalar_tensor_tensor(out=tmp_f, in0=tmp_f, scalar=-1.0, in1=tmp_f, op0=ALU.mult, op1=ALU.max))
            then_wait(v.tensor_scalar(tmp_g, tmp_f, -1.0, 2 * CUTOFF, ALU.mult, ALU.add))
            then_wait(v.tensor_tensor(tmp_f, tmp_f, tmp_g, ALU.min))
            v.sem_inc(angle_ready, 1)
            then_wait(v.tensor_scalar(tmp_j, src_i, P - 1, None, ALU.bitwise_and))
            then_wait(v.tensor_copy(aux[:, :, 1], tmp_j))
            then_wait(v.tensor_copy(aux[:, :, 2].bitcast(I32), dst_i))
            then_wait(v.tensor_tensor(tmp_i, src_i, dst_i, ALU.is_equal))
            then_wait(v.tensor_scalar(tmp_j, dst_i, GW - 1, None, ALU.bitwise_and))
            then_wait(v.scalar_tensor_tensor(out=aux[:, :, 3], in0=tmp_i, scalar=SELF, in1=tmp_j, op0=ALU.mult, op1=ALU.add))
            v.wait_ge(sine_ready, 1)
            then_wait(v.tensor_scalar(tmp_g, tmp_g, 0.5, 0.5, ALU.mult, ALU.add))
            then_wait(v.scalar_tensor_tensor(out=aux[:, :, 0], in0=dist, scalar=CUTOFF, in1=tmp_g, op0=ALU.is_lt, op1=ALU.mult))
            v.wait_ge(small_loaded, SMALL * 16)
            v.wait_ge(types_gathered, NB * 16)
            then_wait(v.tensor_copy(nodes[:, :, :EMB], type_rows[:, :, :EMB]))
            then_wait(v.tensor_copy(emb_rest, type_rows[:, :, EMB:]))
            for k in range(3):
                then_wait(v.tensor_copy(emb_parts[:, :, k * EMB:(k + 1) * EMB], emb_rest))
                if k < 2:
                    then_wait(v.tensor_tensor(emb_rest, emb_rest, emb_parts[:, :, k * EMB:(k + 1) * EMB], ALU.subtract))
            then_wait(v.tensor_tensor(nodes[:, :, HM:HM + H], xs[:, :, :], mult[:, :].unsqueeze(2).to_broadcast([P, NB, H]), ALU.mult))
            then_wait(v.tensor_copy(nodes[:, :, MULT], mult[:, :]))
            v.sem_inc(nodes_ready, 1)
            v.wait_ge(iotas_ready, 1)
            v.wait_ge(hist_ready, 1)
            then_wait(v.tensor_reduce(hist_mask, ident[:, :].rearrange("p (b k) -> p k b", k=4), AX.X, ALU.add))
            then_wait(v.tensor_reduce(fold, ident[:, :].rearrange("p (b k) -> p b k", k=4), AX.X, ALU.add))
            then_wait(v.tensor_tensor(hist_own.rearrange("p (t g) -> p t g", t=4), bk(1, 0, 4 * DG).rearrange("p (t g) -> p t g", t=4),
                                      hist_mask.unsqueeze(2).to_broadcast([P, 4, DG]), ALU.mult))
            then_wait(v.tensor_reduce(hist_part, hist_own.rearrange("p (t g) -> p g t", t=4), AX.X, ALU.add))
            v.sem_inc(own_ready, 1)
            v.wait_ge(hist_folded, 1)
            then_wait(v.tensor_copy(hist_sb[:NB], bk(3, 0, DG, NB)))
            v.sem_inc(hist_copied, 1)
            v.wait_ge(hist_moved, 32)
            then_wait(v.tensor_scalar(row_i[:1], row_f[:1], P - 1.0, None, ALU.add))
            then_wait(v.tensor_scalar(row_i[:1], row_i[:1], 7, None, ALU.logical_shift_right))
            then_wait(v.tensor_copy(row_t[:1], row_i[:1]))
            tiles = row_t[:1].rearrange("a (b g) -> a b g", b=NB)
            start = row_start[:1].rearrange("a (b g) -> a b g", b=NB)
            then_wait(v.tensor_reduce(sb_tiles[:1], tiles, AX.X, ALU.add))
            then_wait(v.tensor_scalar(sb_i[:1], sb_tiles[:1], U - 1.0, float(U), ALU.add, ALU.max))
            then_wait(v.tensor_scalar(sb_i[:1], sb_i[:1], U.bit_length() - 1, None, ALU.logical_shift_right))
            then_wait(v.tensor_scalar(sb_tiles[:1], sb_i[:1], 2.0, None, ALU.max))
            then_wait(v.tensor_tensor_scan(sb_end[:1], ones_row[:1, :NB], sb_tiles[:1], 0.0, ALU.mult, ALU.add))
            then_wait(v.tensor_tensor(sb_first[:1], sb_end[:1], sb_tiles[:1], ALU.subtract))
            then_wait(v.tensor_copy(starts_i[:, :NB], sb_first[:1]))
            then_wait(v.tensor_copy(starts_i[:, NB:], sb_end[:1, NB - 1:]))
            then_wait(v.tensor_scalar(lasts_i[:, :], sb_end[:1], -1.0, None, ALU.add))
            then_wait(v.tensor_scalar(sb_first[:1], sb_first[:1], float(U), None, ALU.mult))
            then_wait(v.tensor_copy(start[:, :, 0], sb_first[:1]))
            for g in range(1, DG):
                then_wait(v.tensor_tensor(start[:, :, g], start[:, :, g - 1], tiles[:, :, g - 1], ALU.add))
            then_wait(v.tensor_scalar(row_f[:1], row_start[:1], float(P), None, ALU.mult))
            v.sem_inc(starts_ready, 1)
            v.wait_ge(bcast_ready, 1)
            then_wait(v.tensor_copy(bin_starts, bk(0, 0, BINS)))
            then_wait(v.tensor_copy(sb_starts, bk(0, BINS, BINS + NB)))
            for c in range(TCOLS):
                then_wait(v.tensor_scalar(small_junk, bin_starts, tile_ids[:, c:c + 1], None, ALU.is_le))
                then_wait(v.tensor_reduce(bin_count[:, c:c + 1], small_junk, AX.X, ALU.add))
                then_wait(v.tensor_scalar(small_junk[:, :NB], sb_starts, tile_ids[:, c:c + 1], None, ALU.is_le))
                then_wait(v.tensor_reduce(sb_count[:, c:c + 1], small_junk[:, :NB], AX.X, ALU.add))
            then_wait(v.scalar_tensor_tensor(out=bin_count, in0=sb_count, scalar=-float(DG), in1=bin_count, op0=ALU.mult, op1=ALU.add))
            then_wait(v.tensor_scalar(bin_count, bin_count, DG - 1.0, None, ALU.add))
            digits = bin_count.rearrange("p (u k) -> p u k", k=U)
            then_wait(v.tensor_copy(unit_f, digits[:, :, U - 1]))
            for k in reversed(range(U - 1)):
                then_wait(v.scalar_tensor_tensor(out=unit_f, in0=unit_f, scalar=8.0, in1=digits[:, :, k], op0=ALU.mult, op1=ALU.add))
            then_wait(v.tensor_copy(unit_i, unit_f))
            v.sem_inc(units_ready, 1)
            def gates_out(g):
                ts = TILES[g]
                return v.tensor_tensor(recs[:, ts[0]:ts[-1] + 1, :H], bk(4 + g % 2, 0, len(ts) * H, EP).rearrange("p (k h) -> p k h", h=H),
                                       b2_all[:EP, :].unsqueeze(1).to_broadcast([EP, len(ts), H]), ALU.add)

            def bin_hots(i, ts):
                for t in ts:
                    v.wait_ge(rank_added, i * BODY + t + 1)
                    v.tensor_scalar(onehot_bin[t % RING], iota_bin[:EP], bin_f[:, bass.ds(i * BODY + t, 1)], None, ALU.is_equal).then_inc(bin_hot, 1)

            for t in TILES[0]:
                v.tensor_scalar(onehot_bin[t], iota_bin[:EP], bin_f[:, t:t + 1], None, ALU.is_equal).then_inc(bin_hot, 1)
            with v.Fori(0, TURNS) as i:
                for g in range(GROUPS):
                    ts = TILES[g]
                    ahead = TILES[g + 1] if g + 1 < GROUPS else range(BODY, BODY + len(TILES[0]))
                    for t in ts:
                        v.wait_ge(rank_ready, i * BODY + t + 1)
                        v.tensor_tensor_reduce(rank_junk[t % 2], bk(6 + t % 2, 0, BINS, EP), onehot_bin[t % RING], 1.0, 0.0, ALU.mult, ALU.add, pos_f[:, t:t + 1]).then_inc(rank_read, 1)
                        if t == ts[min(1, len(ts) - 1)]:
                            bin_hots(i, ahead[:2])
                            v.wait_ge(gate_ready, i * GROUPS + g + 1)
                            gates_out((g - 1) % GROUPS).then_inc(gate_copied, 1)
                    bin_hots(i, ahead[2:])
                    v.wait_ge(scattered[g], i * (16 * len(ts)) + 16)
                    v.sem_inc(v_tick, 1)
                    v.wait_ge(rank_read, i * BODY + ts[-1] + 1)
                    v.tensor_copy(pos_i[g][:, :len(ts)], pos_f[:, ts[0]:ts[-1] + 1])
                    v.tensor_copy(recs[:, ts[0]:ts[-1] + 1, H:], aux[:, bass.ds(i * BODY + ts[0], len(ts)), :])
            v.wait_ge(gate_ready, TURNS * GROUPS + 1)
            gates_out(GROUPS - 1).then_inc(gate_copied, 1)
            v.wait_ge(gate_copied, TURNS * GROUPS + 3)
            v.sem_inc(row_stored_v, 1)

            def hots(q, h):
                v.wait_ge(meta_ready, q * 2 + h + 1)
                for j in range(h * HALF, (h + 1) * HALF):
                    v.tensor_scalar(hot_sh[:, j, :], iota_d[:, :P], meta[:, j, SLOC - H:SLOC - H + 1], None, ALU.is_equal)
                    v.tensor_scalar(hot_d[:, j, :], iota_d[:, :], meta[:, j, DLOC - H:DLOC - H + 1], None, ALU.is_equal).then_inc(hot_ready, 1)

            def messages(q, h):
                js = range(h * HALF, (h + 1) * HALF)
                r = bass.ds(q % 2, 1)
                v.wait_ge(query_ready, q * 2 + h + 1)
                v.sem_inc(v_tick, 1)
                v.wait_ge(emb_ready, q * 2 + h + 2)
                v.sem_inc(v_tick, 1)
                for k, j in enumerate(js):
                    v.tensor_tensor_reduce(adapt_junk[:, k, :, :], bk(7, k * 3 * EMB, (k + 1) * 3 * EMB).rearrange("p (s e) -> p s e", s=3),
                                           query[:, j, :].unsqueeze(1).to_broadcast([P, 3, EMB]), 1.0, 0.0,
                                           ALU.mult, ALU.add, adapt[:, j:j + 1]).then_inc(adapt_done, 1)
                v.wait_ge(adapt_done, q * U + js[-1] + 1 + HALF)
                v.tensor_tensor(gated[:, :, :], rin[:, r, js[0]:js[-1] + 1, :H].rearrange("p r j f -> p (r j) f"),
                                adapt[:, js[0]:js[-1] + 1].unsqueeze(2).to_broadcast([P, HALF, H]), ALU.add).then_inc(gated_ready, 1)
                v.wait_ge(gated_ready, q * 2 + h + 1)
                v.tensor_tensor(msg_pre[:, js[0]:js[-1] + 1, :], gated[:, :, :],
                                ngath[:, r, js[0]:js[-1] + 1, HM:HM + H].rearrange("p r j f -> p (r j) f"), ALU.mult).then_inc(pre_ready, 1)

            v.wait_ge(meta_ready, 1)
            for j in range(HALF):
                v.tensor_scalar(hot_sh[:, j, :], iota_d[:, :P], meta[:, j, SLOC - H:SLOC - H + 1], None, ALU.is_equal)
                v.tensor_scalar(hot_d[:, j, :], iota_d[:, :], meta[:, j, DLOC - H:DLOC - H + 1], None, ALU.is_equal).then_inc(hot_ready, 1)
            with v.Fori(0, NB) as b:
                q0 = v.value_load(starts_i[0:1, bass.ds(b, 1)], min_val=0, max_val=QMAX - 2)
                ql = v.value_load(lasts_i[0:1, bass.ds(b, 1)], min_val=1, max_val=QMAX - 1)
                with v.Fori(q0, ql + 1) as q:
                    hots(q, 1)
                    messages(q, 0)
                    hots(q + 1, 0)
                    messages(q, 1)
                v.wait_ge(summed, ql * U + 2 * U)
                v.sem_inc(v_tick, 1)
                v.tensor_scalar(counts[:, bass.ds(b, 1), CUT:].rearrange("p b d -> p (b d)"), psum[:, CUT:NPAD], 0.5, None, ALU.mult, ALU.add,
                                accum_out=deg2[:, 1, bass.ds(b, 1)])
                v.tensor_copy(agg[:, bass.ds(b, 1), :].rearrange("p b h -> p (b h)"), psum[:, AGG0:AGG0 + H + 1]).then_inc(row_stored_v, 1)

            def bc(a):
                return a.unsqueeze(2).to_broadcast([P, NB, H])

            def all_blocks(a):
                return a[:, :].unsqueeze(1).to_broadcast([P, NB, H])

            roots = 0

            def root():
                nonlocal roots
                roots += 1
                v.sem_inc(var_ready, 1)
                v.wait_ge(std_ready, roots)

            def norm(dst_t, src_t):
                then_wait(v.tensor_reduce(stat_b[:, :], src_t, AX.X, ALU.add))
                then_wait(v.tensor_scalar(stat_b[:, :], stat_b[:, :], 1.0 / H, None, ALU.mult))
                then_wait(v.tensor_tensor(dst_t, src_t, bc(stat_b[:, :]), ALU.subtract))
                then_wait(v.tensor_tensor(square, dst_t, dst_t, ALU.mult))
                then_wait(v.tensor_reduce(stat_b[:, :], square, AX.X, ALU.add))
                then_wait(v.tensor_scalar(stat[:, :], stat_b[:, :], 1.0 / H, LN_EPS, ALU.mult, ALU.add))
                root()
                then_wait(v.reciprocal(stat_b[:, :], std[:, :]))
                then_wait(v.tensor_tensor(dst_t, dst_t, bc(stat_b[:, :]), ALU.mult))

            v.wait_ge(row_stored_v, NB + 1)
            v.wait_ge(row_stored_a, NB + 1)
            then_wait(v.tensor_tensor(dis[:, :], deg2[:, 0, :], deg2[:, 1, :], ALU.add))
            then_wait(v.tensor_scalar(stat[:, :], dis[:, :], 2.0, 1.0, ALU.mult, ALU.max))
            root()
            then_wait(v.reciprocal(stat_b[:, :], std[:, :]))
            then_wait(v.scalar_tensor_tensor(out=dis[:, :], in0=dis[:, :], scalar=0.0, in1=stat_b[:, :], op0=ALU.is_gt, op1=ALU.mult))
            then_wait(v.tensor_scalar(stat_b[:, :], agg[:, :, H], 1e-8, None, ALU.max))
            then_wait(v.reciprocal(stat_b[:, :], stat_b[:, :]))
            then_wait(v.tensor_tensor(work, agg[:, :, :H], bc(stat_b[:, :]), ALU.mult))
            then_wait(v.tensor_tensor(work, work, xs[:, :, :], ALU.add))
            norm(prop, work)
            then_wait(v.tensor_tensor(prop, prop, all_blocks(gamma_all), ALU.mult))
            then_wait(v.tensor_tensor(prop, prop, all_blocks(beta_all), ALU.add))
            then_wait(v.tensor_tensor(work, prop, xs[:, :, :], ALU.add))
            norm(xs[:, :, :], work)

            t3 = orders[:, :, 3, :]
            terms = [xs[:, :, :], t1, t2, t3]
            for k in range(1, ORDERS):
                then_wait(v.tensor_tensor(work, terms[k - 1], bc(dis[:, :]), ALU.mult))
                then_wait(v.tensor_copy(parts[:, :, 0, :], work))
                then_wait(v.tensor_tensor(work, work, parts[:, :, 0, :], ALU.subtract))
                then_wait(v.tensor_copy(parts[:, :, 1, :], work))
                then_wait(v.tensor_tensor(work, work, parts[:, :, 1, :], ALU.subtract))
                then_wait(v.tensor_copy(parts[:, :, 2, :], work))
                v.sem_inc(split_ready, 1)
                with v.Fori(0, NB // 5) as i:
                    for j in range(5):
                        v.wait_ge(prop_ready, i * 5 + (k - 1) * NB + j + 1)
                        v.sem_inc(v_tick, 1)
                        v.tensor_reduce(prop[:, bass.ds(i * 5 + j, 1), :].rearrange("p b h -> p (b h)"),
                                        bk(j, 0, 3 * H).rearrange("p (s h) -> p h s", s=3), AX.X, ALU.add).then_inc(prop_read, 1)
                v.wait_ge(prop_read, k * NB + 5)
                then_wait(v.tensor_tensor(prop, prop, bc(dis[:, :]), ALU.mult))
                if k == 1:
                    then_wait(v.tensor_scalar(t1, prop, -2.0, None, ALU.mult))
                else:
                    then_wait(v.scalar_tensor_tensor(out=terms[k], in0=prop, scalar=-4.0, in1=terms[k - 2], op0=ALU.mult, op1=ALU.subtract))
            v.sem_inc(orders_ready, 1)
            then_wait(v.tensor_tensor(work, xs[:, :, :], all_blocks(bias_all), ALU.add))
            for c in range(-(-NB // 9)):
                lo, hi = 9 * c, min(9 * c + 9, NB)
                v.wait_ge(proj_ready, hi)
                then_wait(v.tensor_tensor(work[:, lo:hi, :], work[:, lo:hi, :], bk(c, 0, (hi - lo) * H).rearrange("p (b h) -> p b h", h=H), ALU.add))
            norm(xs[:, :, :], work)
            v.sem_inc(out_ready, 1)


def kernel(**inputs):
    import numpy as _np
    import concourse.bacc as _bacc
    from concourse import mybir as _mybir
    from concourse.bass_utils import run_bass_kernel_spmd as _run

    nc = _bacc.Bacc("TRN2", target_bir_lowering=False, num_devices=1)
    plan = [("x", 0), ("src", 0), ("dst", 0), ("edge_attr_40", 2), ("edge_weight", 0), ("node_type_119", 0), ("node_vec", 0),
            ("L0_gnn_W1", 1), ("L0_gnn_b1", 0), ("L0_gnn_W2", 1), ("L0_gnn_b2", 0), ("L0_gnn_emb", 1), ("L0_gnn_adaptW", 1),
            ("L0_gnn_gamma", 0), ("L0_gnn_beta", 0), ("L1_gnn_weight", 0), ("L1_gnn_bias", 0)]
    arrays, args = {}, []
    for name, turn in plan:
        a = _np.asarray(inputs[name])
        if turn == 2:
            v = a.reshape(125, 25, 33, -1)
            a = _np.zeros((25, 2, v.shape[3], 17, 125), v.dtype)
            for h in range(2):
                a[:, h, :, :17 - h, :] = v[:, :, h::2].transpose(1, 3, 2, 0)
            a = a.reshape(25, 2 * v.shape[3], 17 * 125)
        a = _np.ascontiguousarray(a.T if turn == 1 else a)
        arrays[f"in_{name}_dram"] = a
        args.append(nc.dram_tensor(f"in_{name}_dram", a.shape, _mybir.dt.from_np(a.dtype), kind="ExternalInput").ap())
    shape = _np.asarray(inputs["x"]).shape
    args.append(nc.dram_tensor("out_0_dram", shape, F32, kind="ExternalOutput").ap())
    gnn_program(nc, *args)
    r = _run(nc, [arrays], core_ids=[0])
    return r.results[0]["out_0_dram"]
```

```python
from contextlib import ExitStack

import concourse.bass as bass
from concourse import mybir

F32 = mybir.dt.float32
F16 = mybir.dt.float16
BF16 = mybir.dt.bfloat16
I32 = mybir.dt.int32
ALU = mybir.AluOpType
ACT = mybir.ActivationFunctionType
AX = mybir.AxisListType

P = 128
PI = 3.141592653589793
CUTOFF = 6.0
LN_EPS = 1e-5


def gnn_program(nc, x, src, dst, edge_attr, edge_weight, node_type, node_vec, w1t, b1, w2t, b2, embt,
                adaptwt, gamma, beta, cheb_w, cheb_bias, out):
    N, H = x.shape
    E, R = dst.shape[0], w1t.shape[0]
    EMB, NEL = embt.shape
    ORDERS = cheb_w.shape[0]
    NB = -(-N // P)
    LAST = N - (NB - 1) * P
    NPAD = NB * P
    GW = 512
    DG = -(-N // GW)
    BINS = NB * DG
    EP = 125
    NT = E // EP
    BODY = 33
    PC = 17
    GROUPS = 9
    TURNS = NT // BODY
    TILES = [range(4 * g, min(4 * g + 4, BODY)) for g in range(GROUPS)]
    COLS = [range(2 * g, min(2 * g + 2, PC)) for g in range(GROUPS)]
    LOADS = [(0, 6, 3), (6, 12, 6), (12, 17, 9)]
    RING = 11
    HT = 4 * (-(-NT // 4))
    HW = 32
    assert EP * NT == E and TURNS * BODY == NT and BODY % RING == 0
    U = 8
    HALF = U // 2
    SLOTS = 4
    TMAX = -(-(-(-E // P) + NB * max(DG + U - 1, 2 * U)) // U) * U + 3 * U
    QMAX = (TMAX // U - 3) | 1
    SPAN = 256
    assert QMAX <= SPAN
    TCOLS = U * (-(-(TMAX + HALF) // P // U))
    PADS = 24
    REC = H + 4
    CW, SLOC, DSTC, DLOC = H, H + 1, H + 2, H + 3
    SELF = 8192.0
    NTAB = 84
    HM, MULT = EMB, EMB + H
    NCH = NB * H
    CUT, CUT_LAST = 4 * GW, 6 * GW

    rec_dram = nc.dram_tensor("rec_sorted", (TMAX * P, REC), F32).ap()
    node_dram = nc.dram_tensor("node_table", (NPAD, NTAB), F32).ap()
    type_dram = nc.dram_tensor("type_table", (NEL, 2 * EMB), F32).ap()
    hist_dram = nc.dram_tensor("hist_row", (1, BINS), F32).ap()
    unit_dram = nc.dram_tensor("unit_row", (1, P * TCOLS // U), I32).ap()

    with ExitStack() as ctx:
        def sb(name, shape, dt=F32):
            return ctx.enter_context(nc.sbuf_tensor(name, shape, dt))

        def sem(name):
            return ctx.enter_context(nc.semaphore(name))

        big = sb("big", [P, NB * NPAD // 2])
        counts = big[:, :].bitcast(F16).rearrange("p (b d) -> p b d", b=NB)
        top = [0]

        def part(n):
            top[0] += n
            assert top[0] <= NB * NPAD // 2
            return big[:, top[0] - n:top[0]]

        src_i = part(NT).bitcast(I32)[:EP]
        dst_i = part(NT).bitcast(I32)[:EP]
        tmp_i = part(NT).bitcast(I32)[:EP]
        tmp_j = part(NT).bitcast(I32)[:EP]
        dist = part(NT)[:EP]
        tmp_f = part(NT)[:EP]
        tmp_g = part(NT)[:EP]
        bin_f = part(NT + len(TILES[0]))[:EP]
        aux = part(NT * 4)[:EP].rearrange("p (t f) -> p t f", f=4)
        attr = part(PC * EP)[:2 * R]
        recs = part(BODY * REC)[:EP].rearrange("p (t f) -> p t f", f=REC)
        hid = [part(2 * EP)[:2 * H] for _ in range(2)]
        onehot_bin = [part(-(-BINS // 2)).bitcast(F16)[:EP, :BINS] for _ in range(RING)]
        pos_f = part(BODY)[:EP]
        pos_i = [part(4).bitcast(I32)[:EP] for _ in range(GROUPS)]
        pad_rec = part(8 * REC)
        iota_bin = part(-(-BINS // 2)).bitcast(F16)[:, :BINS]
        tri_lt = part(P // 2).bitcast(F16)
        tri_ge = part(P // 2).bitcast(F16)
        tri_all = part(P // 2).bitcast(F16)
        onehot_sb = part(HW * HT // 2).bitcast(F16)[:EP].rearrange("p (u b k) -> p u b k", b=HW, k=4)
        started = big[:, top[0] - TCOLS * BINS:top[0]].rearrange("p (t b) -> p t b", t=TCOLS)
        assert TCOLS * BINS <= HW * HT // 2
        onehot_dg = part(DG * HT // 2).bitcast(F16)[:EP].rearrange("p (g t) -> p g t", g=DG)
        hist_mask = part(4)
        hist_own = part(4 * DG)
        hist_part = part(DG)
        fold = part(HW)
        bin_starts = part(BINS)
        sb_starts = part(NB)
        tile_ids = part(TCOLS)
        bin_count = part(TCOLS)
        sb_count = part(TCOLS)
        small_junk = part(BINS)
        unit_f = part(TCOLS // U)
        unit_i = part(TCOLS // U).bitcast(I32)
        ones_row = part(P)
        hist_sb = part(DG)
        row_f = part(BINS)
        row_i = part(BINS).bitcast(I32)
        row_t = part(BINS)
        row_start = part(BINS)
        rank_junk = [small_junk[:EP], row_t[:EP]]
        sb_tiles = part(NB)
        sb_end = part(NB)
        sb_first = part(NB)
        sb_i = part(NB).bitcast(I32)
        types = part(NB).bitcast(I32)
        iota_i = part(GW).bitcast(I32)
        tile_i = part(TCOLS).bitcast(I32)
        sb_h = part(HT // 2).bitcast(F16)[:EP]
        dg_h = part(-(-NT // 2)).bitcast(F16)[:EP, :NT]
        type_rows = part(NB * 2 * EMB).rearrange("p (b f) -> p b f", b=NB)
        nodes = part(NB * NTAB).rearrange("p (b f) -> p b f", b=NB)
        emb_rest = part(NB * EMB).rearrange("p (b e) -> p b e", b=NB)
        type_sb = part(2 * EMB)
        embt_sb = part(NEL)
        adaptwt_sb = part(EMB)

        ident = sb("ident", [P, P])
        ident_h = sb("ident_h", [P, P], F16)
        iota_d = sb("iota_d", [P, GW], F16)
        w1_pair = sb("w1_pair", [2 * R, 2 * H])
        w2_pair = sb("w2_pair", [2 * H, 2 * H])
        b1_pair = sb("b1_pair", [2 * H, 1])
        b2_all = sb("b2_all", [P, H])
        gamma_all = sb("gamma_all", [P, H])
        beta_all = sb("beta_all", [P, H])
        bias_all = sb("bias_all", [P, H])
        xs = sb("xs", [P, NB, H])
        mult = sb("mult", [P, NB])
        turns_i = sb("turns_i", [1, 1], I32)
        spans_i = sb("spans_i", [1, NB], I32)
        unit_row = sb("unit_row_sb", [1, P * TCOLS // U], I32)
        half_pi = sb("half_pi", [P, 1])
        zeros_h = sb("zeros_h", [P, GW], F16)
        cheb_sb = sb("cheb_sb", [2 * H, ORDERS // 2, H])
        agg = sb("agg", [P, NB, H + 1])
        deg_parts = sb("deg_parts", [P, 4, NB])
        dis = sb("dis", [P, NB])
        stat = sb("stat", [P, NB])
        stat_b = sb("stat_b", [P, NB])
        std = sb("std", [P, NB])

        MID = 2 * U * (REC + NTAB) + HALF * H + U * (EMB + 4 + P + P // 2 + GW // 2 + 2 * H + 2) + HALF * P // 2 + HALF * 3 * EMB + 3 * NB * EMB // 2
        STAGED = NB - 5
        mid = sb("mid", [P, max(MID, 4 * NCH + 3 * NCH // 2 + 3 * STAGED * H // 2)])
        used = [0]

        def mid_part(n):
            used[0] += n
            return mid[:, used[0] - n:used[0]]

        rin = mid_part(2 * U * REC).rearrange("p (r j f) -> p r j f", r=2, j=U)
        ngath = mid_part(2 * U * NTAB).rearrange("p (r j f) -> p r j f", r=2, j=U)
        gated = mid_part(HALF * H).rearrange("p (j f) -> p j f", j=HALF)
        query = mid_part(U * EMB).rearrange("p (j f) -> p j f", j=U)
        meta = mid_part(U * 4).rearrange("p (j f) -> p j f", j=U)
        hot_s = mid_part(U * P).rearrange("p (j s) -> p j s", j=U)
        hot_sh = mid_part(U * P // 2).bitcast(F16).rearrange("p (j s) -> p j s", j=U)
        hot_st = mid_part(HALF * P // 2).bitcast(F16).rearrange("p (j s) -> p j s", j=HALF)
        hot_d = mid_part(U * GW // 2).bitcast(F16).rearrange("p (j s) -> p j s", j=U)
        msg_pre = mid_part(U * H).rearrange("p (j s) -> p j s", j=U)
        msg = mid_part(U * (H + 1)).rearrange("p (j s) -> p j s", j=U)
        adapt = mid_part(U)
        adapt_junk = mid_part(HALF * 3 * EMB).rearrange("p (k s e) -> p k s e", k=HALF, s=3)
        emb_parts = mid_part(3 * NB * EMB // 2).bitcast(BF16).rearrange("p (b f) -> p b f", b=NB)
        used[0] = 0

        def node_part(n=NCH):
            return mid_part(n).rearrange("p (b h) -> p b h", b=NB)

        pairs = [mid_part(2 * NCH).rearrange("p (b k h) -> p b k h", b=NB, k=2) for _ in range(ORDERS // 2)]
        terms = [pairs[k // 2][:, :, k % 2, :] for k in range(ORDERS)]
        parts = mid_part(3 * NCH // 2).bitcast(BF16).rearrange("p (b s h) -> p b s h", b=NB, s=3)
        square = mid[:, used[0]:used[0] + NCH].rearrange("p (b h) -> p b h", b=NB)
        staged = mid_part(3 * STAGED * H // 2).bitcast(BF16).rearrange("p (b s h) -> p b s h", b=STAGED, s=3)
        work, prop = agg[:, :, :H], xs[:, :, :]
        turned = [big[:2 * H, j * 2 * P:(j + 1) * 2 * P].rearrange("p (k n) -> p k n", k=2) for j in range(2)]

        psum = ctx.enter_context(nc.psum_tensor("psum", [P, 8 * GW], F32))

        def bk(b, lo, hi, rows=P):
            return psum[:rows, b * GW + lo:b * GW + hi]

        AGG0 = (DG - 1) * GW + P

        small_loaded = sem("small_loaded")
        edges_loaded = sem("edges_loaded")
        v_step = sem("v_step")
        a_step = sem("a_step")
        g_step = sem("g_step")
        iotas_ready = sem("iotas_ready")
        hots_ready = sem("hots_ready")
        hist_ready = sem("hist_ready")
        own_ready = sem("own_ready")
        hist_folded = sem("hist_folded")
        hist_copied = sem("hist_copied")
        hist_moved = sem("hist_moved")
        starts_ready = sem("starts_ready")
        bcast_ready = sem("bcast_ready")
        units_ready = sem("units_ready")
        units_moved = sem("units_moved")
        type_ready = sem("type_ready")
        type_copied = sem("type_copied")
        type_moved = sem("type_moved")
        types_gathered = sem("types_gathered")
        nodes_ready = sem("nodes_ready")
        nodes_moved = sem("nodes_moved")
        angle_ready = sem("angle_ready")
        sine_ready = sem("sine_ready")
        pad_ready = sem("pad_ready")
        attr_loaded = [sem(f"attr_loaded{s}") for s in range(len(LOADS))]
        hid_ready = sem("hid_ready")
        silu_done = sem("silu_done")
        gate_ready = sem("gate_ready")
        gate_copied = sem("gate_copied")
        bin_hot = sem("bin_hot")
        rank_ready = sem("rank_ready")
        rank_read = sem("rank_read")
        rank_added = sem("rank_added")
        pool_tick = sem("pool_tick")
        padded = [sem(f"padded{c}") for c in range(3)]
        scattered = [sem(f"scattered{g}") for g in range(GROUPS)]
        rec_loaded = [sem(f"rec_loaded{s}") for s in range(SLOTS)]
        gathered = [sem(f"gathered{s}") for s in range(SLOTS)]
        loads_over = sem("loads_over")
        recs_in = sem("recs_in")
        rows_in = sem("rows_in")
        meta_ready = sem("meta_ready")
        query_ready = sem("query_ready")
        gated_ready = sem("gated_ready")
        hot_ready = sem("hot_ready")
        counted = sem("counted")
        hot_turned = sem("hot_turned")
        hot_copied = sem("hot_copied")
        emb_ready = sem("emb_ready")
        adapt_done = sem("adapt_done")
        pre_ready = sem("pre_ready")
        msg_ready = sem("msg_ready")
        summed = sem("summed")
        row_stored_v = sem("row_stored_v")
        row_stored_a = sem("row_stored_a")
        agg_stored = sem("agg_stored")
        var_ready = sem("var_ready")
        std_ready = sem("std_ready")
        split_ready = sem("split_ready")
        prop_ready = sem("prop_ready")
        prop_read = sem("prop_read")
        turn_ready = sem("turn_ready")
        turn_copied = sem("turn_copied")
        proj_ready = sem("proj_ready")
        staged_ready = sem("staged_ready")
        parts_moved = sem("parts_moved")
        act_tick = sem("act_tick")
        pe_tick = sem("pe_tick")
        sp_tick = sem("sp_tick")
        v_tick = sem("v_tick")
        orders_ready = sem("orders_ready")
        out_ready = sem("out_ready")
        stored = sem("stored")

        def row_of(v):
            return v.rearrange("(a n) -> a n", a=1)

        xb = x[:(NB - 1) * P].rearrange("(b p) h -> p b h", p=P)
        outb = out[:(NB - 1) * P].rearrange("(b p) h -> p b h", p=P)
        SMALL = 12 + ORDERS // 2 + 6

        def first_and_last(eng, b):
            span = eng.value_load(spans_i[0:1, bass.ds(b, 1)], min_val=0, max_val=SPAN * QMAX - 1)
            return eng.snap(span % SPAN, min_val=0, max_val=QMAX - 1), eng.snap(span // SPAN, min_val=0, max_val=QMAX - 1)

        def pad_out(eng, lo, hi):
            return eng.dma_start(rec_dram[lo * 8 * P:hi * 8 * P].rearrange("(c p k) f -> p c (k f)", p=P, k=8),
                                 pad_rec.unsqueeze(1).to_broadcast([P, hi - lo, 8 * REC]))

        block = ctx.enter_context(nc.Block())

        @block.sync
        def _(sp):
            sp.dma_start(src_i, src.rearrange("(p t) -> p t", p=EP)).then_inc(edges_loaded, 16)
            sp.dma_start(dst_i, dst.rearrange("(p t) -> p t", p=EP)).then_inc(edges_loaded, 16)
            sp.dma_start(dist, edge_weight.rearrange("(p t) -> p t", p=EP)).then_inc(edges_loaded, 16)
            sp.dma_start(embt_sb[:EMB], embt).then_inc(small_loaded, 16)
            sp.dma_start(adaptwt_sb[:EMB], adaptwt).then_inc(small_loaded, 16)
            sp.dma_start(b2_all[:, :], row_of(b2).to_broadcast([P, H])).then_inc(small_loaded, 16)
            sp.dma_start(gamma_all[:, :], row_of(gamma).to_broadcast([P, H])).then_inc(small_loaded, 16)
            sp.dma_start(beta_all[:, :], row_of(beta).to_broadcast([P, H])).then_inc(small_loaded, 16)
            sp.dma_start(bias_all[:, :], row_of(cheb_bias).to_broadcast([P, H])).then_inc(small_loaded, 16)
            for k in range(ORDERS // 2):
                sp.dma_start(cheb_sb[:, k, :], cheb_w[2 * k:2 * k + 2].rearrange("k i o -> (k i) o")).then_inc(small_loaded, 16)
            sp.wait_ge(pad_ready, 1)
            for k in range(2):
                sp.dma_start(w1_pair[k * R:(k + 1) * R, k * H:(k + 1) * H], w1t).then_inc(small_loaded, 16)
                sp.dma_start(w2_pair[k * H:(k + 1) * H, k * H:(k + 1) * H], w2t).then_inc(small_loaded, 16)
                sp.dma_start(b1_pair[k * H:(k + 1) * H, :], b1.rearrange("(h a) -> h a", a=1)).then_inc(small_loaded, 16)
            sp.dma_start(xs[:, :NB - 1, :], xb).then_inc(small_loaded, 16)
            sp.dma_start(xs[:LAST, NB - 1, :], x[(NB - 1) * P:]).then_inc(small_loaded, 16)
            sp.dma_start(mult[:, :NB - 1], node_vec[:(NB - 1) * P].rearrange("(b p) -> p b", p=P),
                         allow_slow_non_contiguous=True).then_inc(small_loaded, 16)
            sp.dma_start(mult[:LAST, NB - 1:NB], node_vec[(NB - 1) * P:].rearrange("(p a) -> p a", a=1)).then_inc(small_loaded, 16)
            sp.dma_start(types[:, :NB - 1], node_type[:(NB - 1) * P].rearrange("(b p) -> p b", p=P),
                         allow_slow_non_contiguous=True).then_inc(small_loaded, 16)
            sp.dma_start(types[:LAST, NB - 1:NB], node_type[(NB - 1) * P:].rearrange("(p a) -> p a", a=1)).then_inc(small_loaded, 16)
            for s, (lo, hi, _) in enumerate(LOADS):
                sp.dma_start(attr[:, lo * EP:hi * EP], edge_attr[0, :, lo * EP:hi * EP]).then_inc(attr_loaded[s], 16)
            sp.wait_ge(type_copied, 1)
            sp.dma_start(type_dram, type_sb[:NEL]).then_inc(type_moved, 16)
            sp.wait_ge(hist_copied, 1)
            sp.dma_start(hist_dram.rearrange("a (b g) -> (a b) g", b=NB), hist_sb[:NB]).then_inc(hist_moved, 16)
            sp.wait_ge(hist_moved, 16)
            sp.dma_start(row_f[:1], hist_dram).then_inc(hist_moved, 16)
            sp.wait_ge(units_ready, 1)
            sp.dma_start(unit_dram.rearrange("a (p c) -> (a p) c", p=P), unit_i).then_inc(units_moved, 16)
            sp.wait_ge(units_moved, 16)
            sp.dma_start(unit_row[:, :], unit_dram).then_inc(units_moved, 16)
            sp.wait_ge(nodes_ready, 1)
            sp.dma_start(node_dram.rearrange("(b p) f -> p b f", p=P), nodes).then_inc(nodes_moved, 16)
            with sp.Fori(1, TURNS) as i:
                for s, (lo, hi, used_by) in enumerate(LOADS):
                    sp.wait_ge(hid_ready, (i - 1) * GROUPS + used_by)
                    sp.dma_start(attr[:, lo * EP:hi * EP], edge_attr[bass.ds(i, 1), :, lo * EP:hi * EP].rearrange("i r e -> (i r) e")).then_inc(attr_loaded[s], 16)
            for g in range(GROUPS):
                sp.wait_ge(scattered[g], 16 + 16 * len(TILES[g]) * TURNS)
            turns = sp.value_load(turns_i[0:1, 0:1], min_val=2 * NB, max_val=QMAX)
            halves = rec_dram.rearrange("(k j p) f -> p k j f", p=P, j=HALF)

            def load(k, slot):
                sp.dma_start(rin[:, slot // 2, slot % 2 * HALF:(slot % 2 + 1) * HALF, :],
                             halves[:, bass.ds(k, 1), :, :].rearrange("p k j f -> p (k j) f")).then_inc(rec_loaded[slot], 16)

            def turn_in(q, use, r):
                for h in range(2):
                    k = 2 * r + h
                    sp.wait_ge(gathered[k], use * (16 * HALF) + 16 * HALF)
                    sp.sem_inc(rows_in, 1)
                    sp.wait_ge(rec_loaded[(k + 2) % SLOTS], use * 16 + 16 * ((k + 2) // SLOTS + 1))
                    sp.sem_inc(recs_in, 1)
                    sp.wait_ge(msg_ready, q * U + (h + 4) * HALF)
                    sp.sem_inc(sp_tick, 1)
                    load(q * 2 + h + 3, (k + 3) % SLOTS)

            for h in range(3):
                load(h, h)
            for h in range(2):
                sp.wait_ge(rec_loaded[h], 16)
                sp.sem_inc(recs_in, 1)
            with sp.Fori(0, turns // 2) as i:
                for r in range(2):
                    turn_in(i * 2 + r, i, r)
            turn_in(turns // 2 * 2, turns // 2, 0)
            sp.wait_ge(rec_loaded[0], turns // 2 * 16 + 32)
            sp.sem_inc(loads_over, 1)
            sp.sem_inc(rows_in, 1)
            sp.wait_ge(out_ready, 1)
            sp.dma_start(outb, xs[:, :NB - 1, :]).then_inc(stored, 16)
            sp.dma_start(out[(NB - 1) * P:], xs[:LAST, NB - 1, :]).then_inc(stored, 16)
            sp.wait_ge(stored, 32)

        @block.gpsimd
        def _(gp):
            n = 0

            def then_wait(inst):
                nonlocal n
                n += 1
                inst.then_inc(g_step, 1)
                gp.wait_ge(g_step, n)

            then_wait(gp.memset(xs[:, NB - 1, :], 0.0))
            then_wait(gp.memset(mult[:, NB - 1:NB], 0.0))
            then_wait(gp.memset(types[:, NB - 1:NB], 0))
            then_wait(gp.memset(pad_rec, 0.0))
            padv = pad_rec.rearrange("p (k f) -> p k f", f=REC)
            then_wait(gp.memset(padv[:, :, SLOC], -1.0))
            then_wait(gp.memset(padv[:, :, DLOC], SELF))
            then_wait(gp.memset(w1_pair[:, :], 0.0))
            then_wait(gp.memset(w2_pair[:, :], 0.0))
            gp.sem_inc(pad_ready, 1)
            then_wait(gp.iota(iota_i, [[1, GW]], base=0, channel_multiplier=0))
            then_wait(gp.tensor_copy(iota_d[:, :], iota_i))
            then_wait(gp.tensor_copy(iota_bin, iota_i[:, :BINS]))
            then_wait(gp.iota(tile_i, [[1, TCOLS]], base=-HALF, channel_multiplier=TCOLS))
            then_wait(gp.tensor_copy(tile_ids, tile_i))
            then_wait(gp.memset(zeros_h[:, :], 0.0))
            then_wait(gp.memset(ones_row, 1.0))
            then_wait(gp.memset(hid[0], 0.0))
            then_wait(gp.memset(nodes[:, :, MULT + 1:], 0.0))
            then_wait(gp.memset(half_pi[:, :], PI / 2))
            then_wait(gp.memset(tri_all, 1.0))
            then_wait(gp.memset(tri_ge, 1.0))
            then_wait(gp.affine_select(tri_lt, tri_ge, [[1, P]], ALU.is_gt, 0.0, base=0, channel_multiplier=-1))
            then_wait(gp.affine_select(tri_ge, tri_ge, [[-1, P]], ALU.is_ge, 0.0, base=0, channel_multiplier=1))
            then_wait(gp.memset(ident[:, :], 1.0))
            then_wait(gp.affine_select(ident[:, :], ident[:, :], [[1, P]], ALU.is_equal, 0.0, base=0, channel_multiplier=-1))
            then_wait(gp.tensor_copy(ident_h[:, :], ident[:, :]))
            gp.sem_inc(iotas_ready, 1)
            for g in range(GROUPS):
                pad_out(gp, g, g + 1).then_inc(scattered[g], 16)
            gp.wait_ge(small_loaded, SMALL * 16)
            gp.wait_ge(type_moved, 16)
            for b in range(NB):
                gp.indirect_dma_start(type_rows[:, b, :], None, type_dram, bass.IndirectOffsetOnAxis(ap=types[:, b:b + 1], axis=0)).then_inc(types_gathered, 16)
            for c in range(3):
                gp.wait_ge(padded[c], 16 * (PADS // 3))
            for g in range(GROUPS):
                gp.wait_ge(scattered[g], 16)
            with gp.Fori(0, TURNS) as i:
                for g in range(GROUPS):
                    gp.wait_ge(gate_copied, i * GROUPS + g + 4)
                    gp.sem_inc(pool_tick, 1)
                    for k, t in enumerate(TILES[g]):
                        gp.indirect_dma_start(rec_dram, bass.IndirectOffsetOnAxis(ap=pos_i[g][:, k:k + 1], axis=0),
                                              recs[:, t, :], None).then_inc(scattered[g], 16)
            gp.wait_ge(nodes_moved, 16)
            gp.wait_ge(starts_ready, 1)
            last = gp.value_load(turns_i[0:1, 0:1], min_val=2 * NB, max_val=QMAX)
            def turn_gathers(q, r):
                for h in range(2):
                    gp.wait_ge(recs_in, q * 2 + h + 1)
                    gp.sem_inc(pool_tick, 1)
                    for j in range(h * HALF, (h + 1) * HALF):
                        gp.indirect_dma_start(ngath[:, r, j, :], None, node_dram, bass.IndirectOffsetOnAxis(ap=rin[:, r, j, DSTC:DSTC + 1].bitcast(I32), axis=0)).then_inc(gathered[2 * r + h], 16)

            with gp.Fori(0, last // 2) as i:
                for r in range(2):
                    turn_gathers(i * 2 + r, r)
            turn_gathers(last // 2 * 2, 0)

        @block.scalar
        def _(act):
            n = 0

            def then_wait(inst):
                nonlocal n
                n += 1
                inst.then_inc(a_step, 1)
                act.wait_ge(a_step, n)

            act.sem_inc(silu_done, 1)
            act.sem_inc(msg_ready, 2 * U)
            act.sem_inc(parts_moved, 1)
            act.wait_ge(pad_ready, 1)

            def fill(c):
                eights = TMAX // 8 - GROUPS
                if c >= 3:
                    act.wait_ge(padded[c % 3], c // 3 * 16)
                pad_out(act, GROUPS + eights * c // PADS, GROUPS + eights * (c + 1) // PADS).then_inc(padded[c % 3], 16)

            for c in range(PADS // 3):
                fill(c)
            act.wait_ge(iotas_ready, 1)
            act.wait_ge(angle_ready, 1)
            act.activation(tmp_g, tmp_f, ACT.Sin, bias=half_pi[:EP, :], scale=-PI / CUTOFF).then_inc(sine_ready, 1)
            act.wait_ge(type_ready, 1)
            then_wait(act.copy(type_sb[:NEL], bk(0, 0, 2 * EMB, NEL)))
            act.sem_inc(type_copied, 1)
            for c in range(PADS // 3, PADS):
                fill(c)
            act.wait_ge(small_loaded, SMALL * 16)
            with act.Fori(0, TURNS) as i:
                for g in range(GROUPS):
                    n1 = len(COLS[g]) * EP
                    act.wait_ge(hid_ready, i * GROUPS + g + 1)
                    act.wait_ge(gate_ready, i * GROUPS + max(g - 1, 0) + 1)
                    act.activation(hid[g % 2][:, :n1], bk(2 + g % 2, 0, n1, 2 * H), ACT.Silu, bias=b1_pair[:, :]).then_inc(silu_done, 1)
            act.sem_inc(row_stored_a, 2)
            act.wait_ge(starts_ready, 1)
            def next_metas(q, h):
                act.wait_ge(recs_in, q * 2 + h + 3)
                act.sem_inc(act_tick, 1)
                act.wait_ge(counted, q * 2 + h + 3)
                act.sem_inc(act_tick, 1)
                act.copy(meta[:, h * HALF:(h + 1) * HALF, :], rin[:, bass.ds((q + 1) % 2, 1), h * HALF:(h + 1) * HALF, H:].rearrange("p r j f -> p (r j) f")).then_inc(meta_ready, 1)

            def turned_out(q, h):
                act.wait_ge(hot_turned, q * 2 + h + 1)
                act.sem_inc(act_tick, 1)
                act.wait_ge(emb_ready, q * 2 + h + 1)
                act.copy(hot_st, bk(7, 0, HALF * P // 2).bitcast(F16).rearrange("p (j s) -> p j s", j=HALF)).then_inc(hot_copied, 1)

            def widen(q, h):
                act.wait_ge(hot_ready, q * U + (h + 1) * HALF)
                act.sem_inc(act_tick, 1)
                act.wait_ge(summed, q * U + (h + 1) * HALF)
                act.copy(hot_s[:, h * HALF:(h + 1) * HALF, :], hot_sh[:, h * HALF:(h + 1) * HALF, :])

            def queries(q, h):
                act.wait_ge(rows_in, q * 2 + h + 1)
                act.sem_inc(act_tick, 1)
                act.wait_ge(msg_ready, q * U + (h + 1) * HALF + U)
                act.sem_inc(act_tick, 1)
                act.copy(query[:, h * HALF:(h + 1) * HALF, :], ngath[:, bass.ds(q % 2, 1), h * HALF:(h + 1) * HALF, :EMB].rearrange("p r j f -> p (r j) f")).then_inc(query_ready, 1)

            def weigh(q, h):
                js = range(h * HALF, (h + 1) * HALF)
                act.wait_ge(pre_ready, q * 2 + h + 1)
                act.sem_inc(act_tick, 1)
                r = bass.ds(q % 2, 1)
                act.copy(msg[:, js[0]:js[-1] + 1, H:], ngath[:, r, js[0]:js[-1] + 1, MULT:MULT + 1].rearrange("p r j f -> p (r j) f"))
                for j in js:
                    act.activation(msg[:, j, :H], msg_pre[:, j, :], ACT.Copy, scale=rin[:, r, j, CW:CW + 1].rearrange("p r f -> p (r f)")).then_inc(msg_ready, 1)

            for h in range(2):
                act.wait_ge(recs_in, h + 1)
                act.copy(meta[:, h * HALF:(h + 1) * HALF, :], rin[:, 0, h * HALF:(h + 1) * HALF, H:]).then_inc(meta_ready, 1)
            act.wait_ge(rows_in, 1)
            act.copy(query[:, :HALF, :], ngath[:, 0, :HALF, :EMB]).then_inc(query_ready, 1)
            act.wait_ge(hot_turned, 1)
            act.wait_ge(emb_ready, 1)
            act.copy(hot_st, bk(7, 0, HALF * P // 2).bitcast(F16).rearrange("p (j s) -> p j s", j=HALF)).then_inc(hot_copied, 1)
            act.wait_ge(hot_ready, HALF)
            act.copy(hot_s[:, :HALF, :], hot_sh[:, :HALF, :])
            with act.Fori(0, NB) as b:
                q0, ql = first_and_last(act, b)
                with act.Fori(q0, ql + 1) as q:
                    next_metas(q, 0)
                    turned_out(q, 1)
                    weigh(q, 0)
                    queries(q, 1)
                    widen(q, 1)
                    next_metas(q, 1)
                    turned_out(q + 1, 0)
                    weigh(q, 1)
                    queries(q + 1, 0)
                    widen(q + 1, 0)
                act.wait_ge(counted, ql * 2 + 4)
                act.sem_inc(act_tick, 1)
                for c in range(2):
                    lo, hi = c * CUT // 2, (c + 1) * CUT // 2
                    act.activation(counts[:, bass.ds(b, 1), lo:hi].rearrange("p b d -> p (b d)"), psum[:, lo:hi], ACT.Copy, scale=0.5,
                                   accum_out=deg_parts[:, c, bass.ds(b, 1)]).then_inc(row_stored_a, 1)
            for k in range(3):
                act.wait_ge(var_ready, k + 1)
                act.activation(std[:, :], stat[:, :], ACT.Sqrt).then_inc(std_ready, 1)
            for k in range(1, ORDERS - 1):
                act.wait_ge(staged_ready, k)
                act.wait_ge(prop_ready, k * NB)
                act.copy(parts[:, :STAGED, :, :].bitcast(F32), staged.bitcast(F32)).then_inc(parts_moved, 1)
            for b in range(NB):
                act.wait_ge(turn_ready, b + 1)
                if b >= 2:
                    act.wait_ge(proj_ready, b - 1)
                act.copy(turned[b % 2], bk(5 + b % 2, 0, 2 * P, 2 * H).rearrange("p (k n) -> p k n", k=2)).then_inc(turn_copied, 1)
            act.wait_ge(var_ready, 4)
            act.activation(std[:, :], stat[:, :], ACT.Sqrt).then_inc(std_ready, 1)

        @block.tensor
        def _(pe):
            pe.sem_inc(rank_added, RING)
            pe.sem_inc(emb_ready, 1)
            pe.sem_inc(summed, U)
            pe.sem_inc(counted, 2)
            pe.wait_ge(iotas_ready, 1)
            pe.wait_ge(small_loaded, SMALL * 16)
            pe.matmul(bk(0, 0, EMB, NEL), embt_sb[:EMB], adaptwt_sb[:EMB], start=True, stop=True)
            pe.transpose(bk(0, EMB, 2 * EMB, NEL), embt_sb[:EMB], ident[:EMB, :EMB]).then_inc(type_ready, 1)
            pe.wait_ge(hots_ready, 1)
            pe.matmul(bk(1, 0, 4 * DG), zeros_h[:, :P], zeros_h[:, :4 * DG], start=True, stop=False, skip_group_check=True)
            for u in range(HT // 4):
                pe.matmul(bk(1, 0, 4 * DG), onehot_sb[:, u, :, :].rearrange("p b k -> p (b k)"),
                          onehot_dg[:, :, u * 4:u * 4 + 4].rearrange("p g t -> p t g"), start=False, stop=False, skip_group_check=True)
            pe.matmul(bk(1, 0, 4 * DG), zeros_h[:, :P], zeros_h[:, :4 * DG], start=False, stop=True, skip_group_check=True).then_inc(hist_ready, 1)
            pe.wait_ge(own_ready, 1)
            pe.matmul(bk(3, 0, DG, HW), fold, hist_part, start=True, stop=True).then_inc(hist_folded, 1)
            pe.wait_ge(starts_ready, 1)
            pe.matmul(bk(0, 0, BINS), ones_row[:1], row_start[:1], start=True, stop=True)
            pe.matmul(bk(0, BINS, BINS + NB), ones_row[:1], sb_first[:1], start=True, stop=True).then_inc(bcast_ready, 1)
            for bank in (6, 7):
                pe.matmul(bk(bank, 0, BINS, EP), ones_row[:1, :EP], row_f[:1], start=True, stop=False, skip_group_check=True)

            def add_bins(bank, edges, t):
                return pe.matmul(bk(bank, 0, BINS, EP), edges[:EP, :EP], onehot_bin[t % RING], start=False, stop=False, skip_group_check=True)

            pe.wait_ge(bin_hot, 1)
            add_bins(6, tri_lt, 0).then_inc(rank_ready, 1)
            add_bins(7, tri_all, 0)
            pe.wait_ge(bin_hot, 2)
            add_bins(7, tri_lt, 1).then_inc(rank_ready, 1)

            with pe.Fori(0, TURNS) as i:
                def even(t):
                    pe.wait_ge(rank_read, i * BODY + t + 1)
                    add_bins(6, tri_ge, t).then_inc(rank_added, 1)
                    if t + 1 < BODY:
                        add_bins(6, tri_all, t + 1)
                    after = t + 2 if t + 1 < BODY else BODY
                    pe.wait_ge(bin_hot, i * BODY + after + 1)
                    add_bins(6, tri_lt, after % BODY).then_inc(rank_ready, 1)

                def odd(t):
                    if t < BODY:
                        pe.wait_ge(rank_read, i * BODY + t + 1)
                        add_bins(7, tri_ge, t).then_inc(rank_added, 1)
                    add_bins(7, tri_all, min(t + 1, BODY) % BODY)
                    if t + 1 != BODY - 1:
                        after = min(t + 2, BODY + 1)
                        pe.wait_ge(bin_hot, i * BODY + after + 1)
                        add_bins(7, tri_lt, after % BODY).then_inc(rank_ready, 1)

                def gate_of(g, c):
                    return pe.matmul(bk(4 + g % 2, c * 2 * H, (c + 1) * 2 * H, EP), hid[g % 2][:, c * EP:(c + 1) * EP], w2_pair[:, :], start=True, stop=True)

                for g in range(GROUPS):
                    ts = TILES[g]
                    last = (g - 1) % GROUPS
                    even(ts[0])
                    odd(ts[0] + 1)
                    pe.wait_ge(silu_done, i * GROUPS + g + 1)
                    pe.sem_inc(pe_tick, 1)
                    pe.wait_ge(gate_copied, i * GROUPS + (max(g - 2, 0) if g else -2) + 3)
                    for c in range(len(COLS[last])):
                        mm = gate_of(last, c)
                    mm.then_inc(gate_ready, 1)
                    if len(ts) > 1:
                        even(ts[2])
                        odd(ts[3])
                    for s, (lo, _, _) in enumerate(LOADS):
                        if COLS[g][0] == lo:
                            pe.wait_ge(attr_loaded[s], i * 16 + 16)
                            pe.sem_inc(pe_tick, 1)
                    pe.wait_ge(silu_done, i * GROUPS + max(g - 1, 0) + 1)
                    n1 = len(COLS[g]) * EP
                    pe.matmul(bk(2 + g % 2, 0, n1, 2 * H), w1_pair[:, :], attr[:, COLS[g][0] * EP:COLS[g][0] * EP + n1], start=True, stop=True).then_inc(hid_ready, 1)
            pe.wait_ge(silu_done, TURNS * GROUPS + 1)
            pe.wait_ge(gate_copied, (TURNS - 1) * GROUPS + GROUPS - 2 + 3)
            pe.matmul(bk(4 + (GROUPS - 1) % 2, 0, 2 * H, EP), hid[(GROUPS - 1) % 2][:, :EP], w2_pair[:, :], start=True, stop=True).then_inc(gate_ready, 1)

            pe.wait_ge(units_moved, 32)
            def turn(q, h):
                pe.wait_ge(hot_ready, q * U + (h + 1) * HALF)
                pe.sem_inc(pe_tick, 1)
                pe.wait_ge(adapt_done, q * U + h * HALF + HALF)
                for k in range(HALF):
                    mm = pe.transpose(bk(7, k * P // 2, (k + 1) * P // 2).bitcast(F16), hot_sh[:, h * HALF + k, :], ident_h[:, :])
                mm.then_inc(hot_turned, 1)

            pe.wait_ge(hot_ready, HALF)
            pe.wait_ge(adapt_done, HALF)
            for k in range(HALF):
                mm = pe.transpose(bk(7, k * P // 2, (k + 1) * P // 2).bitcast(F16), hot_sh[:, k, :], ident_h[:, :])
            mm.then_inc(hot_turned, 1)
            with pe.Fori(0, NB) as b:
                q0, ql = first_and_last(pe, b)
                def groups(q):
                    return pe.value_load(unit_row[0:1, bass.ds(q, 1)], min_val=0, max_val=8 ** U - 1)

                def count(q, h, code):
                    for k in range(HALF):
                        j = h * HALF + k
                        pe.wait_ge(hot_ready, q * U + j + 1)
                        column = pe.snap((code // 8 ** (k + (1 - h) * HALF)) % 8, min_val=0, max_val=DG - 1)
                        mm = pe.matmul(psum[:, bass.ds(column * GW, GW)], hot_sh[:, j, :], hot_d[:, j, :], start=False, stop=False, skip_group_check=True)
                    mm.then_inc(counted, 1)

                def embed(q, h):
                    pe.wait_ge(hot_copied, q * 2 + h + 1)
                    for k in range(HALF):
                        mm = pe.matmul(bk(7, k * 3 * EMB, (k + 1) * 3 * EMB), hot_st[:, k, :],
                                       emb_parts[:, bass.ds(b, 1), :].rearrange("p b e -> p (b e)"), start=True, stop=True)
                    mm.then_inc(emb_ready, 1)

                def add_messages(q, h):
                    for j in range(h * HALF, (h + 1) * HALF):
                        pe.wait_ge(msg_ready, q * U + j + 1 + 2 * U)
                        pe.matmul(psum[:, AGG0:AGG0 + H + 1], hot_s[:, j, :], msg[:, j, :], start=False, stop=False, skip_group_check=True).then_inc(summed, 1)

                embed(q0, 0)
                for stored_by, n, banks in ((row_stored_v, 1, (4, 5)), (row_stored_a, 1, (0, 1)), (row_stored_a, 2, (2, 3)), (row_stored_v, 2, (6,))):
                    pe.wait_ge(stored_by, b * 2 + n)
                    for g in banks:
                        pe.matmul(bk(g, 0, GW), zeros_h[:, :P], zeros_h[:, :], start=True, stop=False, skip_group_check=True)
                count(q0, 0, groups(q0))
                with pe.Fori(q0, ql) as q:
                    code = groups(q + 1)
                    turn(q, 1)
                    count(q, 1, code)
                    embed(q, 1)
                    add_messages(q, 0)
                    turn(q + 1, 0)
                    count(q + 1, 0, code)
                    embed(q + 1, 0)
                    add_messages(q, 1)
                turn(ql, 1)
                count(ql, 1, groups(ql + 1))
                embed(ql, 1)
                add_messages(ql, 0)
                turn(ql + 1, 0)
                add_messages(ql, 1)

            pe.wait_ge(row_stored_v, 2 * NB + 2)
            pe.wait_ge(row_stored_a, 2 * NB + 2)
            with pe.Fori(0, ORDERS - 1) as k:
                pe.wait_ge(split_ready, k + 1)
                pe.wait_ge(parts_moved, k + 1)
                for d in range(NB):
                    pe.wait_ge(prop_read, k * NB + d + 1)
                    for s in range(NB):
                        mm = pe.matmul(bk(d % 5, 0, 3 * H), counts[:, s, d * P:(d + 1) * P], parts[:, s, :, :].rearrange("p s h -> p (s h)"), start=(s == 0), stop=(s == NB - 1))
                    mm.then_inc(prop_ready, 1)
            pe.wait_ge(orders_ready, 1)
            for b in range(NB + 1):
                if b < NB:
                    if b >= 2:
                        pe.wait_ge(turn_copied, b - 1)
                    for k in range(2):
                        mm = pe.transpose(bk(5 + b % 2, k * P, (k + 1) * P, 2 * H), pairs[k][:, b, :, :].rearrange("p k h -> p (k h)"), ident[:, :])
                    mm.then_inc(turn_ready, 1)
                if b > 0:
                    c, o = (b - 1) // 9, (b - 1) % 9 * H
                    pe.wait_ge(turn_copied, b)
                    pe.matmul(bk(c, o, o + H), turned[(b - 1) % 2][:, 0, :], cheb_sb[:, 0, :], start=True, stop=False)
                    pe.matmul(bk(c, o, o + H), turned[(b - 1) % 2][:, 1, :], cheb_sb[:, 1, :], start=False, stop=True).then_inc(proj_ready, 1)

        @block.vector
        def _(v):
            n = 0

            def then_wait(inst):
                nonlocal n
                n += 1
                inst.then_inc(v_step, 1)
                v.wait_ge(v_step, n)

            v.sem_inc(gate_copied, 2)
            v.sem_inc(adapt_done, HALF)
            v.sem_inc(prop_read, 5)
            v.wait_ge(edges_loaded, 3 * 16)
            v.memset(onehot_sb[:, :, NB:, :], 0.0)
            then_wait(v.memset(onehot_dg[:, :, NT:], 0.0))
            then_wait(v.tensor_scalar(tmp_i, src_i, 7, None, ALU.logical_shift_right))
            then_wait(v.tensor_scalar(tmp_j, dst_i, 9, None, ALU.logical_shift_right))
            v.memset(sb_h[:, NT:], -1.0)
            then_wait(v.tensor_copy(sb_h[:, :NT], tmp_i))
            then_wait(v.tensor_copy(dg_h, tmp_j))
            for b in range(NB):
                v.tensor_scalar(onehot_sb[:, :, b, :], sb_h.rearrange("p (u k) -> p u k", k=4), float(b), None, ALU.is_equal)
            for g in range(DG - 1):
                v.tensor_scalar(onehot_dg[:, g, :NT], dg_h, float(g), None, ALU.is_equal)
            then_wait(v.tensor_scalar(onehot_dg[:, DG - 1, :NT], dg_h, float(DG - 1), None, ALU.is_equal))
            v.sem_inc(hots_ready, 1)
            then_wait(v.memset(bin_f[:, NT:], -1.0))
            then_wait(v.scalar_tensor_tensor(out=bin_f[:, :NT], in0=tmp_i, scalar=float(DG), in1=tmp_j, op0=ALU.mult, op1=ALU.add))
            then_wait(v.scalar_tensor_tensor(out=tmp_g, in0=dist, scalar=-1.0, in1=dist, op0=ALU.mult, op1=ALU.max))
            then_wait(v.tensor_scalar(tmp_i, tmp_g, 1.0 / (2 * CUTOFF), None, ALU.mult))
            then_wait(v.scalar_tensor_tensor(out=tmp_f, in0=tmp_i, scalar=-2 * CUTOFF, in1=tmp_g, op0=ALU.mult, op1=ALU.add))
            then_wait(v.scalar_tensor_tensor(out=tmp_f, in0=tmp_f, scalar=-1.0, in1=tmp_f, op0=ALU.mult, op1=ALU.max))
            then_wait(v.tensor_scalar(tmp_g, tmp_f, -1.0, 2 * CUTOFF, ALU.mult, ALU.add))
            then_wait(v.tensor_tensor(tmp_f, tmp_f, tmp_g, ALU.min))
            v.sem_inc(angle_ready, 1)
            then_wait(v.tensor_scalar(tmp_j, src_i, P - 1, None, ALU.bitwise_and))
            then_wait(v.tensor_copy(aux[:, :, 1], tmp_j))
            then_wait(v.tensor_copy(aux[:, :, 2].bitcast(I32), dst_i))
            then_wait(v.tensor_tensor(tmp_i, src_i, dst_i, ALU.is_equal))
            then_wait(v.tensor_scalar(tmp_j, dst_i, GW - 1, None, ALU.bitwise_and))
            then_wait(v.scalar_tensor_tensor(out=aux[:, :, 3], in0=tmp_i, scalar=SELF, in1=tmp_j, op0=ALU.mult, op1=ALU.add))
            v.wait_ge(sine_ready, 1)
            then_wait(v.tensor_scalar(tmp_g, tmp_g, 0.5, 0.5, ALU.mult, ALU.add))
            then_wait(v.scalar_tensor_tensor(out=aux[:, :, 0], in0=dist, scalar=CUTOFF, in1=tmp_g, op0=ALU.is_lt, op1=ALU.mult))
            v.wait_ge(iotas_ready, 1)
            v.wait_ge(hist_ready, 1)
            then_wait(v.tensor_reduce(hist_mask, ident[:, :].rearrange("p (b k) -> p k b", k=4), AX.X, ALU.add))
            then_wait(v.tensor_reduce(fold, ident[:, :].rearrange("p (b k) -> p b k", k=4), AX.X, ALU.add))
            then_wait(v.tensor_tensor(hist_own.rearrange("p (t g) -> p t g", t=4), bk(1, 0, 4 * DG).rearrange("p (t g) -> p t g", t=4),
                                      hist_mask.unsqueeze(2).to_broadcast([P, 4, DG]), ALU.mult))
            then_wait(v.tensor_reduce(hist_part, hist_own.rearrange("p (t g) -> p g t", t=4), AX.X, ALU.add))
            v.sem_inc(own_ready, 1)
            v.wait_ge(hist_folded, 1)
            then_wait(v.tensor_copy(hist_sb[:NB], bk(3, 0, DG, NB)))
            v.sem_inc(hist_copied, 1)
            v.wait_ge(hist_moved, 32)
            then_wait(v.tensor_scalar(row_i[:1], row_f[:1], P - 1.0, None, ALU.add))
            then_wait(v.tensor_scalar(row_i[:1], row_i[:1], 7, None, ALU.logical_shift_right))
            then_wait(v.tensor_copy(row_t[:1], row_i[:1]))
            tiles = row_t[:1].rearrange("a (b g) -> a b g", b=NB)
            start = row_start[:1].rearrange("a (b g) -> a b g", b=NB)
            then_wait(v.tensor_reduce(sb_tiles[:1], tiles, AX.X, ALU.add))
            then_wait(v.tensor_scalar(sb_i[:1], sb_tiles[:1], U - 1.0, float(U), ALU.add, ALU.max))
            then_wait(v.tensor_scalar(sb_i[:1], sb_i[:1], U.bit_length() - 1, None, ALU.logical_shift_right))
            then_wait(v.tensor_scalar(sb_tiles[:1], sb_i[:1], 2.0, None, ALU.max))
            then_wait(v.tensor_tensor_scan(sb_end[:1], ones_row[:1, :NB], sb_tiles[:1], 0.0, ALU.mult, ALU.add))
            then_wait(v.tensor_tensor(sb_first[:1], sb_end[:1], sb_tiles[:1], ALU.subtract))
            then_wait(v.tensor_copy(turns_i[:, :], sb_end[:1, NB - 1:]))
            then_wait(v.tensor_scalar(turns_i[:, :], turns_i[:, :], 1, None, ALU.bitwise_or))
            then_wait(v.tensor_copy(sb_end[:1, NB - 1:], turns_i[:, :]))
            then_wait(v.tensor_scalar(sb_end[:1], sb_end[:1], -1.0, float(SPAN), ALU.add, ALU.mult))
            then_wait(v.tensor_tensor(spans_i[:, :], sb_end[:1], sb_first[:1], ALU.add))
            then_wait(v.tensor_scalar(sb_first[:1], sb_first[:1], float(U), None, ALU.mult))
            then_wait(v.tensor_copy(start[:, :, 0], sb_first[:1]))
            for g in range(1, DG):
                then_wait(v.tensor_tensor(start[:, :, g], start[:, :, g - 1], tiles[:, :, g - 1], ALU.add))
            then_wait(v.tensor_scalar(row_f[:1], row_start[:1], float(P), None, ALU.mult))
            v.sem_inc(starts_ready, 1)
            v.wait_ge(bcast_ready, 1)
            then_wait(v.tensor_copy(bin_starts, bk(0, 0, BINS)))
            then_wait(v.tensor_copy(sb_starts, bk(0, BINS, BINS + NB)))
            for starts, n_starts, count in ((bin_starts, BINS, bin_count), (sb_starts, NB, sb_count)):
                before = started[:, :, :n_starts]
                then_wait(v.tensor_tensor(before, starts.unsqueeze(1).to_broadcast([P, TCOLS, n_starts]),
                                          tile_ids.unsqueeze(2).to_broadcast([P, TCOLS, n_starts]), ALU.is_le))
                then_wait(v.tensor_reduce(count, before, AX.X, ALU.add))
            then_wait(v.scalar_tensor_tensor(out=bin_count, in0=sb_count, scalar=-float(DG), in1=bin_count, op0=ALU.mult, op1=ALU.add))
            then_wait(v.tensor_scalar(bin_count, bin_count, DG - 1.0, None, ALU.add))
            digits = bin_count.rearrange("p (u k) -> p u k", k=U)
            then_wait(v.tensor_copy(unit_f, digits[:, :, U - 1]))
            for k in reversed(range(U - 1)):
                then_wait(v.scalar_tensor_tensor(out=unit_f, in0=unit_f, scalar=8.0, in1=digits[:, :, k], op0=ALU.mult, op1=ALU.add))
            then_wait(v.tensor_copy(unit_i, unit_f))
            v.sem_inc(units_ready, 1)
            v.wait_ge(small_loaded, SMALL * 16)
            v.wait_ge(types_gathered, NB * 16)
            then_wait(v.tensor_copy(nodes[:, :, :EMB], type_rows[:, :, :EMB]))
            then_wait(v.tensor_copy(emb_rest, type_rows[:, :, EMB:]))
            for k in range(3):
                then_wait(v.tensor_copy(emb_parts[:, :, k * EMB:(k + 1) * EMB], emb_rest))
                if k < 2:
                    then_wait(v.tensor_tensor(emb_rest, emb_rest, emb_parts[:, :, k * EMB:(k + 1) * EMB], ALU.subtract))
            then_wait(v.tensor_tensor(nodes[:, :, HM:HM + H], xs[:, :, :], mult[:, :].unsqueeze(2).to_broadcast([P, NB, H]), ALU.mult))
            then_wait(v.tensor_copy(nodes[:, :, MULT], mult[:, :]))
            v.sem_inc(nodes_ready, 1)
            def gates_out(g):
                ts = TILES[g]
                return v.tensor_tensor(recs[:, ts[0]:ts[-1] + 1, :H], bk(4 + g % 2, 0, len(ts) * H, EP).rearrange("p (k h) -> p k h", h=H),
                                       b2_all[:EP, :].unsqueeze(1).to_broadcast([EP, len(ts), H]), ALU.add)

            def bin_hots(i, ts):
                for t in ts:
                    v.wait_ge(rank_added, i * BODY + t + 1)
                    v.tensor_scalar(onehot_bin[t % RING], iota_bin[:EP], bin_f[:, bass.ds(i * BODY + t, 1)], None, ALU.is_equal).then_inc(bin_hot, 1)

            for t in TILES[0]:
                v.tensor_scalar(onehot_bin[t], iota_bin[:EP], bin_f[:, t:t + 1], None, ALU.is_equal).then_inc(bin_hot, 1)
            with v.Fori(0, TURNS) as i:
                for g in range(GROUPS):
                    ts = TILES[g]
                    ahead = TILES[g + 1] if g + 1 < GROUPS else range(BODY, BODY + len(TILES[0]))
                    for t in ts:
                        v.wait_ge(rank_ready, i * BODY + t + 1)
                        v.tensor_tensor_reduce(rank_junk[t % 2], bk(6 + t % 2, 0, BINS, EP), onehot_bin[t % RING], 1.0, 0.0, ALU.mult, ALU.add, pos_f[:, t:t + 1]).then_inc(rank_read, 1)
                        if t == ts[min(1, len(ts) - 1)]:
                            bin_hots(i, ahead[:2])
                            v.wait_ge(gate_ready, i * GROUPS + g + 1)
                            gates_out((g - 1) % GROUPS).then_inc(gate_copied, 1)
                    bin_hots(i, ahead[2:])
                    v.wait_ge(scattered[g], i * (16 * len(ts)) + 16)
                    v.sem_inc(v_tick, 1)
                    v.wait_ge(rank_read, i * BODY + ts[-1] + 1)
                    v.tensor_copy(pos_i[g][:, :len(ts)], pos_f[:, ts[0]:ts[-1] + 1])
                    v.tensor_copy(recs[:, ts[0]:ts[-1] + 1, H:], aux[:, bass.ds(i * BODY + ts[0], len(ts)), :])
            v.wait_ge(gate_ready, TURNS * GROUPS + 1)
            gates_out(GROUPS - 1).then_inc(gate_copied, 1)
            v.wait_ge(gate_copied, TURNS * GROUPS + 3)
            v.sem_inc(row_stored_v, 2)

            def hots(q, h):
                v.wait_ge(meta_ready, q * 2 + h + 1)
                for j in range(h * HALF, (h + 1) * HALF):
                    v.tensor_scalar(hot_sh[:, j, :], iota_d[:, :P], meta[:, j, SLOC - H:SLOC - H + 1], None, ALU.is_equal)
                    v.tensor_scalar(hot_d[:, j, :], iota_d[:, :], meta[:, j, DLOC - H:DLOC - H + 1], None, ALU.is_equal).then_inc(hot_ready, 1)

            def messages(q, h):
                js = range(h * HALF, (h + 1) * HALF)
                r = bass.ds(q % 2, 1)
                v.wait_ge(query_ready, q * 2 + h + 1)
                v.sem_inc(v_tick, 1)
                v.wait_ge(emb_ready, q * 2 + h + 2)
                v.sem_inc(v_tick, 1)
                for k, j in enumerate(js):
                    v.tensor_tensor_reduce(adapt_junk[:, k, :, :], bk(7, k * 3 * EMB, (k + 1) * 3 * EMB).rearrange("p (s e) -> p s e", s=3),
                                           query[:, j, :].unsqueeze(1).to_broadcast([P, 3, EMB]), 1.0, 0.0,
                                           ALU.mult, ALU.add, adapt[:, j:j + 1]).then_inc(adapt_done, 1)
                v.wait_ge(adapt_done, q * U + js[-1] + 1 + HALF)
                v.tensor_tensor(gated[:, :, :], rin[:, r, js[0]:js[-1] + 1, :H].rearrange("p r j f -> p (r j) f"),
                                adapt[:, js[0]:js[-1] + 1].unsqueeze(2).to_broadcast([P, HALF, H]), ALU.add).then_inc(gated_ready, 1)
                v.wait_ge(gated_ready, q * 2 + h + 1)
                v.tensor_tensor(msg_pre[:, js[0]:js[-1] + 1, :], gated[:, :, :],
                                ngath[:, r, js[0]:js[-1] + 1, HM:HM + H].rearrange("p r j f -> p (r j) f"), ALU.mult).then_inc(pre_ready, 1)

            v.wait_ge(meta_ready, 1)
            for j in range(HALF):
                v.tensor_scalar(hot_sh[:, j, :], iota_d[:, :P], meta[:, j, SLOC - H:SLOC - H + 1], None, ALU.is_equal)
                v.tensor_scalar(hot_d[:, j, :], iota_d[:, :], meta[:, j, DLOC - H:DLOC - H + 1], None, ALU.is_equal).then_inc(hot_ready, 1)
            with v.Fori(0, NB) as b:
                q0, ql = first_and_last(v, b)
                with v.Fori(q0, ql + 1) as q:
                    hots(q, 1)
                    messages(q, 0)
                    hots(q + 1, 0)
                    messages(q, 1)
                v.wait_ge(counted, ql * 2 + 4)
                v.sem_inc(v_tick, 1)
                v.tensor_scalar(counts[:, bass.ds(b, 1), CUT:CUT_LAST].rearrange("p b d -> p (b d)"), psum[:, CUT:CUT_LAST], 0.5, None, ALU.mult, ALU.add,
                                accum_out=deg_parts[:, 2, bass.ds(b, 1)]).then_inc(row_stored_v, 1)
                v.wait_ge(summed, ql * U + 2 * U)
                v.sem_inc(v_tick, 1)
                v.tensor_scalar(counts[:, bass.ds(b, 1), CUT_LAST:].rearrange("p b d -> p (b d)"), psum[:, CUT_LAST:NPAD], 0.5, None, ALU.mult, ALU.add,
                                accum_out=deg_parts[:, 3, bass.ds(b, 1)])
                v.tensor_copy(agg[:, bass.ds(b, 1), :].rearrange("p b h -> p (b h)"), psum[:, AGG0:AGG0 + H + 1]).then_inc(row_stored_v, 1)

            def bc(a):
                return a.unsqueeze(2).to_broadcast([P, NB, H])

            def all_blocks(a):
                return a[:, :].unsqueeze(1).to_broadcast([P, NB, H])

            roots = 0

            def root():
                nonlocal roots
                roots += 1
                v.sem_inc(var_ready, 1)
                v.wait_ge(std_ready, roots)

            def norm(dst_t, src_t):
                then_wait(v.tensor_reduce(stat_b[:, :], src_t, AX.X, ALU.add))
                then_wait(v.tensor_scalar(stat_b[:, :], stat_b[:, :], 1.0 / H, None, ALU.mult))
                then_wait(v.tensor_tensor(dst_t, src_t, bc(stat_b[:, :]), ALU.subtract))
                then_wait(v.tensor_tensor(square, dst_t, dst_t, ALU.mult))
                then_wait(v.tensor_reduce(stat_b[:, :], square, AX.X, ALU.add))
                then_wait(v.tensor_scalar(stat[:, :], stat_b[:, :], 1.0 / H, LN_EPS, ALU.mult, ALU.add))
                root()
                then_wait(v.reciprocal(stat_b[:, :], std[:, :]))
                then_wait(v.tensor_tensor(dst_t, dst_t, bc(stat_b[:, :]), ALU.mult))

            v.wait_ge(row_stored_v, 2 * NB + 2)
            v.wait_ge(row_stored_a, 2 * NB + 2)
            v.wait_ge(loads_over, 1)
            then_wait(v.tensor_reduce(dis[:, :], deg_parts[:, :, :].rearrange("p c b -> p b c"), AX.X, ALU.add))
            then_wait(v.tensor_scalar(stat[:, :], dis[:, :], 2.0, 1.0, ALU.mult, ALU.max))
            root()
            then_wait(v.reciprocal(stat_b[:, :], std[:, :]))
            then_wait(v.scalar_tensor_tensor(out=dis[:, :], in0=dis[:, :], scalar=0.0, in1=stat_b[:, :], op0=ALU.is_gt, op1=ALU.mult))
            temp = terms[1]
            then_wait(v.tensor_scalar(stat_b[:, :], agg[:, :, H], 1e-8, None, ALU.max))
            then_wait(v.reciprocal(stat_b[:, :], stat_b[:, :]))
            then_wait(v.tensor_tensor(work, work, bc(stat_b[:, :]), ALU.mult))
            then_wait(v.tensor_tensor(work, work, xs[:, :, :], ALU.add))
            norm(temp, work)
            then_wait(v.tensor_tensor(temp, temp, all_blocks(gamma_all), ALU.mult))
            then_wait(v.tensor_tensor(temp, temp, all_blocks(beta_all), ALU.add))
            then_wait(v.tensor_tensor(work, temp, xs[:, :, :], ALU.add))
            norm(terms[0], work)

            def split(term, lo, hi, out):
                rest = work[:, lo:hi, :]
                then_wait(v.tensor_tensor(rest, term[:, lo:hi, :], dis[:, lo:hi].unsqueeze(2).to_broadcast([P, hi - lo, H]), ALU.mult))
                for s in range(3):
                    then_wait(v.tensor_copy(out[:, lo:hi, s, :], rest))
                    if s < 2:
                        then_wait(v.tensor_tensor(rest, rest, out[:, lo:hi, s, :], ALU.subtract))

            split(terms[0], 0, NB, parts)
            v.sem_inc(split_ready, 1)
            for k in range(1, ORDERS):
                for lo in range(0, NB, 5):
                    hi = lo + 5
                    for d in range(lo, hi):
                        v.wait_ge(prop_ready, (k - 1) * NB + d + 1)
                        v.tensor_reduce(prop[:, d, :], bk(d % 5, 0, 3 * H).rearrange("p (s h) -> p h s", s=3), AX.X, ALU.add).then_inc(prop_read, 1)
                    v.wait_ge(prop_read, (k - 1) * NB + hi + 5)
                    then_wait(v.tensor_tensor(prop[:, lo:hi, :], prop[:, lo:hi, :], dis[:, lo:hi].unsqueeze(2).to_broadcast([P, 5, H]), ALU.mult))
                    if k == 1:
                        then_wait(v.tensor_scalar(terms[1][:, lo:hi, :], prop[:, lo:hi, :], -2.0, None, ALU.mult))
                    else:
                        then_wait(v.scalar_tensor_tensor(out=terms[k][:, lo:hi, :], in0=prop[:, lo:hi, :], scalar=-4.0, in1=terms[k - 2][:, lo:hi, :], op0=ALU.mult, op1=ALU.subtract))
                    if k < ORDERS - 1:
                        if lo == 0:
                            v.wait_ge(parts_moved, k)
                        split(terms[k], lo, hi, staged if lo < STAGED else parts)
                        if hi == STAGED:
                            v.sem_inc(staged_ready, 1)
                if k < ORDERS - 1:
                    v.sem_inc(split_ready, 1)
            v.sem_inc(orders_ready, 1)
            then_wait(v.tensor_tensor(work, terms[0], all_blocks(bias_all), ALU.add))
            for c in range(-(-NB // 9)):
                lo, hi = 9 * c, min(9 * c + 9, NB)
                v.wait_ge(proj_ready, hi)
                then_wait(v.tensor_tensor(work[:, lo:hi, :], work[:, lo:hi, :], bk(c, 0, (hi - lo) * H).rearrange("p (b h) -> p b h", h=H), ALU.add))
            norm(xs[:, :, :], work)
            v.sem_inc(out_ready, 1)


def kernel(**inputs):
    import numpy as _np
    import concourse.bacc as _bacc
    from concourse import mybir as _mybir
    from concourse.bass_utils import run_bass_kernel_spmd as _run

    nc = _bacc.Bacc("TRN2", target_bir_lowering=False, num_devices=1)
    plan = [("x", 0), ("src", 0), ("dst", 0), ("edge_attr_40", 2), ("edge_weight", 0), ("node_type_119", 0), ("node_vec", 0),
            ("L0_gnn_W1", 1), ("L0_gnn_b1", 0), ("L0_gnn_W2", 1), ("L0_gnn_b2", 0), ("L0_gnn_emb", 1), ("L0_gnn_adaptW", 1),
            ("L0_gnn_gamma", 0), ("L0_gnn_beta", 0), ("L1_gnn_weight", 0), ("L1_gnn_bias", 0)]
    arrays, args = {}, []
    for name, turn in plan:
        a = _np.asarray(inputs[name])
        if turn == 2:
            v = a.reshape(125, 25, 33, -1)
            a = _np.zeros((25, 2, v.shape[3], 17, 125), v.dtype)
            for h in range(2):
                a[:, h, :, :17 - h, :] = v[:, :, h::2].transpose(1, 3, 2, 0)
            a = a.reshape(25, 2 * v.shape[3], 17 * 125)
        a = _np.ascontiguousarray(a.T if turn == 1 else a)
        arrays[f"in_{name}_dram"] = a
        args.append(nc.dram_tensor(f"in_{name}_dram", a.shape, _mybir.dt.from_np(a.dtype), kind="ExternalInput").ap())
    shape = _np.asarray(inputs["x"]).shape
    args.append(nc.dram_tensor("out_0_dram", shape, F32, kind="ExternalOutput").ap())
    gnn_program(nc, *args)
    r = _run(nc, [arrays], core_ids=[0])
    return r.results[0]["out_0_dram"]
```
